# Optimizing a Trainium2 kernel written in Bass

```python
import numpy as np
import jax
import jax.numpy as jnp

def _softmax(x, axis=-1):
    return jax.nn.softmax(x, axis=axis)

def _gelu(x):
    return jax.nn.gelu(x, approximate=True)

def _silu(x):
    return jax.nn.silu(x)

def _sigmoid(x):
    return jax.nn.sigmoid(x)

def _layernorm(x, axis=-1, eps=1e-05):
    m = jnp.mean(x, axis=axis, keepdims=True)
    v = jnp.var(x, axis=axis, keepdims=True)
    return (x - m) / jnp.sqrt(v + eps)

def _scatter_add(tgt, idx, src, axis=0):
    return tgt.at[idx].add(src)

def _segment_sum(src, seg, n):
    return jax.ops.segment_sum(src, seg, n)
kernel_name = 'mk_xattn_ffn_d1_seqx_r8_43a415'

def setup_inputs(seed: int=0):
    np.random.seed(seed)
    _w = jnp.asarray

    def _rec_inputs():
        import jax
        import jax.numpy as jnp
        _rk = jax.random.key(seed)
        x = -0.0002928 + 1 * jax.random.normal(jax.random.fold_in(_rk, 1), (128, 64, 128), jnp.float32)
        _lenS = 64 - jax.random.randint(jax.random.fold_in(_rk, 7), (128,), 0, max(1, 64 // 4) + 1, jnp.int32)
        _lenS2 = 64 - jax.random.randint(jax.random.fold_in(_rk, 8), (128,), 0, max(1, 64 // 4) + 1, jnp.int32)
        _ctx_1024P = jax.random.normal(jax.random.fold_in(_rk, 11), (128, 16, 128), jnp.float32)
        _ctx_1024c = jax.random.dirichlet(jax.random.fold_in(_rk, 511), 0.3 * jnp.ones((16,), jnp.float32), (128, 64))
        _ctx_1024t = jnp.einsum('bsk,bkd->bsd', _ctx_1024c, _ctx_1024P)
        _ctx_1024t = _ctx_1024t * jax.lax.rsqrt(jnp.mean(jnp.square(_ctx_1024t)) + 1e-12) * 0.953939
        ctx_1024 = -1.39393e-06 + 0.999914 * (_ctx_1024t + 0.3 * jax.random.normal(jax.random.fold_in(_rk, 611), (128, 64, 128), jnp.float32))
        return (x, ctx_1024)
    x, ctx_1024 = _rec_inputs()

    def _L0_xattn_setup():
        import jax, jax.numpy as jnp
        import numpy as np
        D_MODEL = 128
        NUM_HEADS = 16
        D_K = D_MODEL // NUM_HEADS

        def _split_heads(x, B, S):
            return x.reshape(B, S, NUM_HEADS, D_K).transpose(0, 2, 1, 3)
        key = jax.random.key(seed)
        ks = jax.random.split(key, 12)
        B, S, D = (2, 256, D_MODEL)
        s = 1.0 / np.sqrt(D)
        inp = {'Q': jax.random.normal(ks[0], (B, S, D), jnp.float32), 'K': jax.random.normal(ks[1], (B, S, D), jnp.float32), 'V': jax.random.normal(ks[2], (B, S, D), jnp.float32), 'Wq': jax.random.normal(ks[3], (D, D), jnp.float32) * s, 'bq': jax.random.normal(ks[4], (D,), jnp.float32) * s, 'Wk': jax.random.normal(ks[5], (D, D), jnp.float32) * s, 'bk': jax.random.normal(ks[6], (D,), jnp.float32) * s, 'Wv': jax.random.normal(ks[7], (D, D), jnp.float32) * s, 'bv': jax.random.normal(ks[8], (D,), jnp.float32) * s, 'Wo': jax.random.normal(ks[9], (D, D), jnp.float32) * s, 'bo': jax.random.normal(ks[10], (D,), jnp.float32) * s}
        return inp
    _L0_xattn_all = _L0_xattn_setup()
    _L0_xattn_in = {k: v for k, v in _L0_xattn_all.items() if k in ('Wq', 'bq', 'Wk', 'bk', 'Wv', 'bv', 'Wo', 'bo')}
    del _L0_xattn_all

    def _L0_ffn_setup():
        import jax, jax.numpy as jnp
        import numpy as np
        D_MODEL, D_FF, N_EXP = (128, 512, 8)
        key = jax.random.key(seed)
        ks = jax.random.split(key, 8)
        s = lambda fan_in: 1.0 / np.sqrt(fan_in)
        x = jax.random.normal(ks[0], (4, 256, D_MODEL), dtype=jnp.float32)
        Wr = jax.random.uniform(ks[1], (N_EXP, D_MODEL), jnp.float32, -s(D_MODEL), s(D_MODEL))
        br = jax.random.uniform(ks[2], (N_EXP,), jnp.float32, -s(D_MODEL), s(D_MODEL))
        W1 = jax.random.uniform(ks[3], (N_EXP, D_FF, D_MODEL), jnp.float32, -s(D_MODEL), s(D_MODEL))
        b1 = jax.random.uniform(ks[4], (N_EXP, D_FF), jnp.float32, -s(D_MODEL), s(D_MODEL))
        W2 = jax.random.uniform(ks[5], (N_EXP, D_MODEL, D_FF), jnp.float32, -s(D_FF), s(D_FF))
        b2 = jax.random.uniform(ks[6], (N_EXP, D_MODEL), jnp.float32, -s(D_FF), s(D_FF))
        return {'x': x, 'Wr': Wr, 'br': br, 'W1': W1, 'b1': b1, 'W2': W2, 'b2': b2}
    _L0_ffn_all = _L0_ffn_setup()
    _L0_ffn_in = {k: v for k, v in _L0_ffn_all.items() if k in ('Wr', 'br', 'W1', 'b1', 'W2', 'b2')}
    del _L0_ffn_all
    return {'x': x, 'ctx_1024': ctx_1024, 'L0_xattn_Wq': _L0_xattn_in['Wq'], 'L0_xattn_bq': _L0_xattn_in['bq'], 'L0_xattn_Wk': _L0_xattn_in['Wk'], 'L0_xattn_bk': _L0_xattn_in['bk'], 'L0_xattn_Wv': _L0_xattn_in['Wv'], 'L0_xattn_bv': _L0_xattn_in['bv'], 'L0_xattn_Wo': _L0_xattn_in['Wo'], 'L0_xattn_bo': _L0_xattn_in['bo'], 'L0_ffn_Wr': _L0_ffn_in['Wr'], 'L0_ffn_br': _L0_ffn_in['br'], 'L0_ffn_W1': _L0_ffn_in['W1'], 'L0_ffn_b1': _L0_ffn_in['b1'], 'L0_ffn_W2': _L0_ffn_in['W2'], 'L0_ffn_b2': _L0_ffn_in['b2']}

def reference(x, ctx_1024, L0_xattn_Wq, L0_xattn_bq, L0_xattn_Wk, L0_xattn_bk, L0_xattn_Wv, L0_xattn_bv, L0_xattn_Wo, L0_xattn_bo, L0_ffn_Wr, L0_ffn_br, L0_ffn_W1, L0_ffn_b1, L0_ffn_W2, L0_ffn_b2):
    import jax
    import jax.numpy as jnp

    def _L0_xattn_ref(Q, K, V, Wq, bq, Wk, bk, Wv, bv, Wo, bo):
        import jax, jax.numpy as jnp
        import numpy as np
        D_MODEL = 128
        NUM_HEADS = 16
        D_K = D_MODEL // NUM_HEADS

        def _split_heads(x, B, S):
            return x.reshape(B, S, NUM_HEADS, D_K).transpose(0, 2, 1, 3)
        B, S, D = Q.shape
        q = _split_heads(Q @ Wq.T + bq, B, S)
        k = _split_heads(K @ Wk.T + bk, B, S)
        v = _split_heads(V @ Wv.T + bv, B, S)
        scale = 1.0 / np.sqrt(D_K).astype(np.float32)
        scores = jnp.einsum('bhqd,bhkd->bhqk', q, k) * scale
        probs = jax.nn.softmax(scores, axis=-1)
        out = jnp.einsum('bhqk,bhkd->bhqd', probs, v)
        out = out.transpose(0, 2, 1, 3).reshape(B, S, D)
        return out @ Wo.T + bo

    def _L0_ffn_ref(x, Wr, br, W1, b1, W2, b2):
        import jax, jax.numpy as jnp
        import numpy as np
        D_MODEL, D_FF, N_EXP = (128, 512, 8)
        B, S, D = x.shape
        xf = x.reshape(-1, D)
        logits = xf @ Wr.T + br
        expert_idx = jnp.argmax(logits, axis=-1)
        h = jax.nn.relu(jnp.einsum('td,efd->etf', xf, W1) + b1[:, None, :])
        y = jnp.einsum('etf,edf->etd', h, W2) + b2[:, None, :]
        out = y[expert_idx, jnp.arange(xf.shape[0])]
        return out.reshape(B, S, D)
    x = x + _L0_xattn_ref(_layernorm(x, axis=-1), ctx_1024, ctx_1024, L0_xattn_Wq, L0_xattn_bq, L0_xattn_Wk, L0_xattn_bk, L0_xattn_Wv, L0_xattn_bv, L0_xattn_Wo, L0_xattn_bo)
    x = x + _L0_ffn_ref(_layernorm(x, axis=-1), L0_ffn_Wr, L0_ffn_br, L0_ffn_W1, L0_ffn_b1, L0_ffn_W2, L0_ffn_b2)
    return x

_drawn_inputs = setup_inputs


def setup_inputs(seed=0):
    import zlib

    import numpy as np

    out = dict(_drawn_inputs(seed))
    spreads = {}
    factors = {'L0_xattn_bk': 8.0, 'L0_ffn_b1': 3.258}
    for name, (base, spread) in spreads.items():
        noise = np.random.default_rng([zlib.crc32(name.encode()), seed]).standard_normal(out[name].shape)
        drawn = base * np.exp(spread * noise) if base else spread * noise
        out[name] = jnp.asarray(drawn.astype(out[name].dtype))
    for name, factor in factors.items():
        out[name] = (out[name] * factor).astype(out[name].dtype)
    return out
```

```python
import concourse.bass as bass
from concourse import mybir
from contextlib import ExitStack
import numpy as np

P = 128
D = 128
SEQ = 64
BATCH = 128
TOK = BATCH * SEQ
NT = TOK // P
GT = 4
NG = NT // GT
GW = GT * P
H = 16
DK = D // H
HP = H // 2
E = 8
F = 512
FC = F // P
CAP = TOK + P
NB = TOK // P + E
PADS = NB - TOK // P
ROWS = E * CAP + PADS * P
KR = 4
RW = 2 * D + 4
ID = 2 * D
EPS = 1e-5
SCALE = float(1.0 / np.sqrt(np.float32(DK)))

C_ID, C_TRI, C_ONE, C_OB, C_JM, C_PREF, C_BASE, C_LIM, C_BLK, C_EPS, C_END = np.cumsum(
    [0, P, P, P, 2 * 32, 4 * SEQ, E, E, NT, NB, 1]).tolist()


def constants():
    c = np.zeros((P, C_END), np.float32)
    p = np.arange(P)
    c[:, C_ID:C_ID + P] = np.eye(P)
    c[:, C_TRI:C_TRI + P] = p[:, None] < p[None, :]
    c[:, C_ONE:C_ONE + P] = 1
    for s in range(2):
        for r in range(2):
            a = C_OB + 32 * s + 16 * s + DK * r
            c[SEQ * r:SEQ * r + SEQ, a:a + DK] = 1
    for j in range(4):
        c[(p // DK) % 4 == j, C_JM + SEQ * j:C_JM + SEQ * (j + 1)] = 1
    c[:, C_PREF:C_PREF + E] = E - np.arange(E)
    c[:, C_BASE:C_BASE + E] = CAP * np.arange(E)
    c[:, C_LIM:C_LIM + NT] = P * np.arange(NT)
    c[:, C_BLK:C_BLK + NB] = np.arange(NB)
    c[:, C_EPS] = EPS
    pad = np.zeros((P, RW), np.float32)
    pad[:, ID] = np.full(P, TOK, np.int32).view(np.float32)
    ids = np.ascontiguousarray(np.arange(TOK, dtype=np.int32).reshape(NT, P).T)
    return c, pad, ids


class Step:

    def __init__(self, it, r, ring):
        self.it, self.r, self.ring = it, r, ring
        self.n = it * ring + r

    def back(self, k):
        q, r = divmod(self.r - k, self.ring)
        return Step(self.it + q if q else self.it, r, self.ring)


def need(eng, sem, value):
    if not isinstance(value, int) or value > 0:
        eng.wait_ge(sem, value)


def steps(eng, first, last, ring, body, peel=0, tail=0):
    lo = -(-max(first, peel) // ring)
    hi = (last - tail) // ring
    for n in range(first, lo * ring):
        body(Step(n // ring, n % ring, ring))
    if hi - lo > 1:
        with eng.Fori(lo, hi) as it:
            for r in range(ring):
                body(Step(it, r, ring))
    else:
        hi = lo
    for n in range(hi * ring, last):
        body(Step(n // ring, n % ring, ring))


def build(nc, x, ctxT, wq, wk, wv, wo, bq, bk, bv, bo, wr, br, w1, b1, w2, b2, con, pad, ids, out):
    f32, i32 = mybir.dt.float32, mybir.dt.int32
    ALU, ACT, AX = mybir.AluOpType, mybir.ActivationFunctionType, mybir.AxisListType
    x_v = x.rearrange("(t p) d -> p t d", p=P)
    rows = nc.dram_tensor("rows", (ROWS, RW), f32).ap()

    ctx = ExitStack()
    with ctx:
        def sb(name, *shape, dt=f32):
            return ctx.enter_context(nc.sbuf_tensor(name, list(shape), dt))

        def sem(name):
            return ctx.enter_context(nc.semaphore(name))

        def sems(name, n):
            return [sem(f"{name}{i}") for i in range(n)]

        X = sb("X", P, NT, D)
        BIG = sb("BIG", P, 3 * TOK)
        QT = BIG[:, 0:TOK]
        KT = BIG[:, TOK:2 * TOK]
        V = BIG[:, 2 * TOK:3 * TOK]
        C = sb("C", P, C_END)
        ident, tri, ones = C[:, C_ID:C_ID + P], C[:, C_TRI:C_TRI + P], C[:, C_ONE:C_ONE + P]
        WQ, WK, WV, WO = (sb(n, P, D) for n in ("WQ", "WK", "WV", "WO"))
        BV, BO = sb("BV", P, D), sb("BO", P, D)
        BQK = sb("BQK", P, 2)
        WR, BR = sb("WR", P, E), sb("BR", P, E)
        STAT = sb("STAT", P, GT, 6)
        MS = sb("MS", P, 4, GT)
        MV = sb("MV", P, 2, 2, GT)
        SD = sb("SD", P, 2, GT)
        RSTD = sb("RSTD", P, GT)
        QS = sb("QS", P, KR, P)
        KJ = sb("KJ", P, KR, 2, 4, SEQ)
        KM = sb("KM", P, KR, 2, H, SEQ)
        SB = sb("SB", P, 2, H * SEQ)
        MX = sb("MX", P, 2, H)
        PT = sb("PT", P, 2, HP, P)
        XN = SB[:].rearrange("p r (t d) -> p (r t) d", d=D)[:, 0:2 * GT, :].rearrange("p (r t) d -> p r t d", r=2)
        XNT = SB[:, 1, :].rearrange("p (r w) -> p r w", r=2)
        CT = PT[:, 0].rearrange("p (r a) d -> p r (a d)", r=2)
        VP = sb("VP", P, 2, 2, HP, 32)
        RD = sb("RD", P, P)
        OT = sb("OT", P, 2, P)

        def big(at, *shape):
            n = int(np.prod(shape))
            v = BIG[:, at:at + n]
            if len(shape) == 2:
                v = v.rearrange("p (a b) -> p a b", a=shape[0])
            if len(shape) == 3:
                v = v.rearrange("p (a b c) -> p a b c", a=shape[0], b=shape[1])
            return v, at + n

        at = 0
        RG, at = big(at, 2, GT, RW)
        X1T, at = big(at, 2, GW)
        LG, at = big(at, GT, E)
        TOP, at = big(at, GT)
        HOT, at = big(at, 2, GT, E)
        PREF, at = big(at, GT, E)
        BASE, at = big(at, GT + 1, E)
        POS, at = big(at, GT, E)
        DEST, at = big(at, GT)
        PADR, at = big(at, RW)
        CMP, at = big(at, NB * E)
        TE, at = big(at, 6, E)
        TB, at = big(at, 4, NB)
        W2, at = big(at, E, FC, D)
        B1, at = big(at, E, FC)
        B2, at = big(at, E, D)
        W1, at = big(at, 4, F)
        RT, at = big(at, 4, RW)
        XT, at = big(at, 2, P)
        HT, at = big(at, 2, F)
        YO, at = big(at, 4, D)
        assert at <= 3 * TOK
        IDS = sb("IDS", P, NT, dt=i32)
        DESTI = sb("DESTI", P, 2, GT, dt=i32)
        TABI = sb("TABI", 1, 2, NB, dt=i32)
        CNTI = sb("CNTI", 1, E, dt=i32)

        PS = ctx.enter_context(nc.psum_tensor("PS", [P, 8 * 512], f32))

        def bank(k, n=1):
            return PS[:, 512 * k:512 * (k + n)]

        con_in, con2_in, w2_in = sem("con_in"), sem("con2_in"), sem("w2_in")
        x_in, ct_in = sems("x_in", 2), sems("ct_in", 2)
        stat_done, mv_done, sd_done, rstd_done, xn_done = (sem(n) for n in ("stat_done", "mv_done", "sd_done", "rstd_done", "xn_done"))
        xt_done, xnt_ready = sem("xt_done"), sem("xnt_ready")
        q_done, k_done, v_done = sem("q_done"), sem("k_done"), sem("v_done")
        q_kept, k_kept, v_kept = sem("q_kept"), sem("k_kept"), sem("v_kept")
        bo_mm, bo_ready, xb_done = sem("bo_mm"), sem("bo_ready"), sem("xb_done")
        zeroed = sem("zeroed")
        qs_in, km_in = sems("qs_in", KR), sems("km_in", KR)
        kj_done, vp_done = sem("kj_done"), sem("vp_done")
        s_done, mx_done, sub_done, exp_done = (sem(n) for n in ("s_done", "mx_done", "sub_done", "exp_done"))
        pt_done, pt_ready, od_done, rd_done, ot_ready = (sem(n) for n in ("pt_done", "pt_ready", "od_done", "rd_done", "ot_ready"))
        wo_done, x1_done = sem("wo_done"), sem("x1_done")
        half_done, gap_done, half2, gap2 = (sem(n) for n in ("half_done", "gap_done", "half2", "gap2"))
        stat2, mv2, sd2, rstd2, xn2 = (sem(n) for n in ("stat2", "mv2", "sd2", "rstd2", "xn2"))
        x1c_done, id_done, xt2_done, x1t_ready = (sem(n) for n in ("x1c_done", "id_done", "xt2_done", "x1t_ready"))
        lg_done, lg_ready, top_done, eq_done, pref_done, best_done, hot_done = (
            sem(n) for n in ("lg_done", "lg_ready", "top_done", "eq_done", "pref_done", "best_done", "hot_done"))
        rank_done, base_step, pos_done, posm_done, dest_done, desti_done = (
            sem(n) for n in ("rank_done", "base_step", "pos_done", "posm_done", "dest_done", "desti_done"))
        base_carry = sem("base_carry")
        routed, sent = sems("routed", 2), sem("sent")
        padr_in, pads_out, pad_out = sem("padr_in"), sem("pads_out"), sem("pad_out")
        cnt_ready, tab_step, tab_ready = sem("cnt_ready"), sem("tab_step"), sem("tab_ready")
        rt_in, w1_in, y_out = sems("rt_in", 4), sems("w1_in", 4), sems("y_out", 4)
        bx_done, bxt_ready, h_done, hb_done, h_ready = (sem(n) for n in ("bx_done", "bxt_ready", "h_done", "hb_done", "h_ready"))
        y_done, yx_done, yo_ready = sem("y_done"), sem("yx_done"), sem("yo_ready")

        block = ctx.enter_context(nc.Block())

        @block.sync
        def _(sp):
            for dst, src in ((C[:], con), (WQ[:], wq), (WK[:], wk), (WV[:], wv), (BQK[:, 0:1], bq),
                             (BQK[:, 1:2], bk), (WO[:], wo), (BV[:], bv), (BO[:], bo), (WR[:], wr),
                             (BR[:], br), (IDS[:], ids)):
                sp.dma_start(dst, src).then_inc(con_in, 16)

            def load_group(s):
                def go(before):
                    if before:
                        sp.wait_ge(stat_done, s.n - 1)
                    sp.dma_start(X[:, bass.ds(s.n * GT, GT), :], x_v[:, bass.ds(s.n * GT, GT), :]).then_inc(x_in[s.r], 16)
                    if before:
                        sp.wait_ge(v_done, s.n - 1)
                        sp.wait_ge(k_done, s.n - 1)
                    sp.dma_start(CT[:, s.r, :], ctxT[:, bass.ds(s.n * GW, GW)]).then_inc(ct_in[s.r], 16)
                go(not isinstance(s.n, int) or s.n >= 2)
            steps(sp, 0, NG, 2, load_group, peel=2)

            sp.wait_ge(q_kept, NG)
            sp.wait_ge(zeroed, 2)
            def spread(s):
                need(sp, s_done, s.n - KR + 1)
                sp.dma_start(QS[:, s.r, :], QT[:, bass.ds(s.n * P, P)]).then_inc(qs_in[s.r], 16)
                sp.wait_ge(kj_done, s.n + 1)
                for g in range(4):
                    r = slice(32 * g, 32 * g + 32)
                    sp.dma_start(KM[r, s.r, :, 4 * g:4 * g + 4, :], KJ[r, s.r]).then_inc(km_in[s.r], 16)
            steps(sp, 0, NT, KR, spread, peel=4)

            sp.wait_ge(vp_done, NT)
            for r in range(KR):
                sp.wait_ge(qs_in[r], 16 * (NT // KR))
            sp.dma_start(PADR[:], pad).then_inc(padr_in, 16)
            sp.dma_start(W2[:], w2).then_inc(w2_in, 16)
            sp.dma_start(B1[:], b1).then_inc(w2_in, 16)
            sp.dma_start(B2[:], b2).then_inc(w2_in, 16)
            sp.wait_ge(padr_in, 16)
            for k in range(PADS):
                sp.dma_start(rows[E * CAP + k * P:E * CAP + (k + 1) * P, :], PADR[:]).then_inc(pads_out, 16)
            sp.wait_ge(cnt_ready, 1)
            for e in range(E):
                end = sp.value_load(CNTI[0:1, e:e + 1], min_val=0, max_val=ROWS - P)
                sp.dma_start(rows[bass.ds(end, P), :], PADR[:]).then_inc(pads_out, 16)

            sp.wait_ge(tab_ready, 1)
            sp.wait_ge(pads_out, 16 * (PADS + E))
            for r in range(2):
                sp.wait_ge(routed[r], 16 * GT * (NG // 2))
            def load_block(s):
                row = sp.value_load(TABI[0:1, 0, bass.ds(s.n, 1)], min_val=0, max_val=ROWS - P)
                ex = sp.value_load(TABI[0:1, 1, bass.ds(s.n, 1)], min_val=0, max_val=E - 1)
                need(sp, h_done, s.n - 3)
                sp.dma_start(W1[:, s.r, :], w1[:, bass.ds(ex * F, F)]).then_inc(w1_in[s.r], 16)
                need(sp, y_out[s.r], 16 * s.it)
                sp.dma_start(RT[:, s.r, :], rows[bass.ds(row, P), :]).then_inc(rt_in[s.r], 16)
            steps(sp, 0, NB, 4, load_block, peel=4)

        @block.gpsimd
        def _(pool):
            nc.gpsimd.memset(KM[:], 0.0).then_inc(zeroed, 1)
            nc.gpsimd.memset(VP[:], 0.0).then_inc(zeroed, 1)

            pool.wait_ge(bo_ready, 1)
            def add_bias(s):
                pool.wait_ge(xn_done, s.n + 1)
                g = X[:, bass.ds(s.n * GT, GT), :]
                nc.gpsimd.tensor_tensor(g, g, BO[:].unsqueeze(1).to_broadcast([P, GT, D]), ALU.add).then_inc(xb_done, 1)
            steps(pool, 0, NG, 2, add_bias)

            jmask = C[:, C_JM:C_JM + 4 * SEQ].rearrange("p (j k) -> p j k", j=4)
            pool.wait_ge(k_kept, NG)
            pool.wait_ge(v_kept, NG)
            pool.wait_ge(zeroed, 2)
            def masks(s):
                whole = not isinstance(s.n, int)
                if whole or s.n < NT:
                    need(pool, km_in[s.r], 64 * s.it)
                    for b in range(2):
                        k = KT[:, bass.ds(s.n * P + SEQ * b, SEQ)].unsqueeze(1).to_broadcast([P, 4, SEQ])
                        last = nc.gpsimd.tensor_tensor(KJ[:, s.r, b], k, jmask, ALU.mult)
                    last.then_inc(kj_done, 1)
                if whole or s.n >= 3:
                    t = s.back(3)
                    need(pool, od_done, t.n - 1)
                    for z in range(2):
                        dst = VP[:, t.r % 2].rearrange("p b (c z) m -> p (b c) z m", z=2)[:, :, z, 16 * z:16 * z + 16].rearrange("p g (r w) -> p g r w", w=DK)
                        v = V[:, bass.ds(t.n * P, P)].rearrange("p (g z w) -> p g z w", z=2, w=DK)[:, :, z, :].unsqueeze(2).to_broadcast([P, 8, 2, DK])
                        own = C[:, C_OB:C_OB + 16].rearrange("p (r w) -> p r w", w=DK).unsqueeze(1).to_broadcast([P, 8, 2, DK])
                        last = nc.gpsimd.tensor_tensor(dst, v, own, ALU.mult)
                    last.then_inc(vp_done, 1)
            steps(pool, 0, NT + 3, KR, masks, peel=8, tail=3)

            last_row, last_token = pool.to_reg(ROWS - 1), pool.to_reg(TOK - 1)
            def route(s):
                need(pool, routed[s.r], 16 * GT * s.it)
                nc.gpsimd.tensor_copy(RG[:, s.r, :, ID:ID + 1].bitcast(i32), IDS[:, bass.ds(s.n * GT, GT)].unsqueeze(2)).then_inc(id_done, 1)
                pool.wait_ge(id_done, s.n + 1)
                pool.wait_ge(desti_done, s.n + 1)
                pool.wait_ge(x1c_done, s.n + 1)
                pool.sem_inc(sent, 1)
                for t in range(GT):
                    nc.gpsimd.indirect_dma_start(
                        out=rows, out_offset=bass.IndirectOffsetOnAxis(ap=DESTI[:, s.r, t:t + 1], axis=0),
                        in_=RG[:, s.r, t, :], in_offset=None, bounds_check=last_row, oob_is_err=False).then_inc(routed[s.r], 16)
            pool.wait_ge(x1_done, NT)
            for r in range(KR):
                pool.wait_ge(qs_in[r], 16 * (NT // KR))
            steps(pool, 0, NG, 2, route, peel=2)

            def home(s):
                pool.wait_ge(yo_ready, s.n + 1)
                pool.sem_inc(sent, 1)
                nc.gpsimd.indirect_dma_start(
                    out=out, out_offset=bass.IndirectOffsetOnAxis(ap=RT[:, s.r, ID:ID + 1].bitcast(i32), axis=0),
                    in_=YO[:, s.r, :], in_offset=None, bounds_check=last_token, oob_is_err=False).then_inc(y_out[s.r], 16)
            steps(pool, 0, NB, 4, home)
            for r in range(4):
                pool.wait_ge(y_out[r], 16 * (NB // 4))

        @block.scalar
        def _(act):
            act.wait_ge(con_in, 16 * 12)

            def root(s, mv, sd, rstd):
                need(act, rstd, s.n - 1)
                act.wait_ge(mv, s.n + 1)
                nc.scalar.activation(SD[:, s.r, :], MV[:, s.r, 1, :], ACT.Sqrt, bias=C[:, C_EPS:C_EPS + 1]).then_inc(sd, 1)

            def keep(t):
                whole = not isinstance(t.n, int)
                if whole or t.n < NG:
                    root(t, mv_done, sd_done, rstd_done)
                if not whole and t.n < 1:
                    return
                s = t.back(1)
                act.wait_ge(xt_done, s.n + 1)
                need(act, q_done, s.n - 1)
                nc.scalar.copy(XNT[:, s.r, :], bank(s.r)).then_inc(xnt_ready, 1)
                act.wait_ge(k_done, s.n + 1)
                nc.scalar.activation(KT[:, bass.ds(s.n * GW, GW)], bank(4 + s.r), ACT.Identity, bias=BQK[:, 1:2]).then_inc(k_kept, 1)
                act.wait_ge(q_done, s.n + 1)
                nc.scalar.activation(QT[:, bass.ds(s.n * GW, GW)], bank(2 + s.r), ACT.Identity, bias=BQK[:, 0:1]).then_inc(q_kept, 1)
            steps(act, 0, NG + 1, 2, keep, peel=4, tail=1)

            def softmax(s):
                if isinstance(s.n, int) and s.n >= NT:
                    pass
                else:
                    act.wait_ge(sub_done, s.n + 1)
                    nc.scalar.activation(SB[:, s.r, :], SB[:, s.r, :], ACT.Exp, scale=SCALE).then_inc(exp_done, 1)
                if isinstance(s.n, int) and s.n < 1:
                    return
                b = s.back(1)
                act.wait_ge(pt_done, b.n + 1)
                need(act, od_done, b.n - 1)
                nc.scalar.copy(PT[:, b.r].rearrange("p a b -> p (a b)"), bank(4, 2)).then_inc(pt_ready, 1)
            steps(act, 0, NT + 1, 2, softmax, peel=4, tail=1)

            act.wait_ge(x1_done, NT)
            for r in range(KR):
                act.wait_ge(qs_in[r], 16 * (NT // KR))
            def stage3(t):
                whole = not isinstance(t.n, int)
                if whole or t.n < NG:
                    root(t, mv2, sd2, rstd2)
                if not whole and t.n < 1:
                    return
                s = t.back(1)
                need(act, routed[s.r], 16 * GT * s.it)
                nc.scalar.copy(RG[:, s.r, :, D:2 * D], X[:, bass.ds(s.n * GT, GT), :]).then_inc(x1c_done, 1)
                act.wait_ge(xt2_done, s.n + 1)
                need(act, lg_done, s.n - 1)
                nc.scalar.copy(X1T[:, s.r, :], bank(s.r)).then_inc(x1t_ready, 1)
            steps(act, 0, NG + 1, 2, stage3, peel=4, tail=1)

            def ffn(s):
                if not (isinstance(s.n, int) and s.n >= NB):
                    act.wait_ge(bx_done, s.n + 1)
                    need(act, h_done, s.n - 1)
                    nc.scalar.copy(XT[:, s.r % 2, :], bank(s.r % 2)[:, 0:P]).then_inc(bxt_ready, 1)
                if isinstance(s.n, int) and s.n < 1:
                    return
                b = s.back(1)
                act.wait_ge(hb_done, b.n + 1)
                nc.scalar.activation(HT[:, b.r % 2, :], HT[:, b.r % 2, :], ACT.Relu).then_inc(h_ready, 1)
            act.wait_ge(lg_done, NG)
            steps(act, 0, NB + 1, 4, ffn, peel=4, tail=1)

        @block.vector
        def _(dve):
            dve.wait_ge(con_in, 16 * 12)
            dve.wait_ge(bo_mm, 1)
            nc.vector.tensor_tensor(BO[:], bank(0)[:, 0:D], BO[:], ALU.add).then_inc(bo_ready, 1)

            def moments(src, s, stat, half, gap, mv, done):
                n = s.n
                need(dve, half, n)
                need(dve, mv, n)
                for t in range(GT):
                    last = nc.vector.bn_stats(STAT[:, t, :], src(t))
                last.then_inc(stat, 1)
                dve.wait_ge(stat, n + 1)
                m0, m1, v0, v1 = (STAT[:, :, k] for k in (1, 4, 2, 5))
                nc.vector.tensor_tensor(MS[:, 0, :], m0, m1, ALU.add)
                nc.vector.tensor_tensor(MS[:, 1, :], v0, v1, ALU.add)
                nc.vector.tensor_tensor(MS[:, 2, :], m0, m1, ALU.subtract).then_inc(half, 1)
                dve.wait_ge(half, n + 1)
                need(dve, done, n - 1)
                nc.vector.tensor_scalar(MV[:, s.r, 0, :], MS[:, 0, :], 0.5, None, ALU.mult)
                nc.vector.scalar_tensor_tensor(MS[:, 3, :], MS[:, 2, :], 0.25, MS[:, 2, :], ALU.mult, ALU.mult).then_inc(gap, 1)
                dve.wait_ge(gap, n + 1)
                nc.vector.scalar_tensor_tensor(MV[:, s.r, 1, :], MS[:, 1, :], 1.0 / D, MS[:, 3, :], ALU.mult, ALU.add).then_inc(mv, 1)

            def normalise(src, dst, s, sd, rstd, done):
                n = s.n
                need(dve, done, n)
                dve.wait_ge(sd, n + 1)
                nc.vector.reciprocal(RSTD[:], SD[:, s.r, :]).then_inc(rstd, 1)
                dve.wait_ge(rstd, n + 1)
                for t in range(GT):
                    last = nc.vector.tensor_scalar(dst(t), src(t), MV[:, s.r, 0, t:t + 1], RSTD[:, t:t + 1], ALU.subtract, ALU.mult)
                last.then_inc(done, 1)

            def stage1(s):
                whole = not isinstance(s.n, int)
                if whole or s.n < NG:
                    dve.wait_ge(x_in[s.r], 16 * (s.it + 1))
                    xg = X[:, bass.ds(s.n * GT, GT), :]
                    moments(lambda t: xg[:, t, :], s, stat_done, half_done, gap_done, mv_done, xn_done)
                if whole or 1 <= s.n < NG + 1:
                    b = s.back(1)
                    need(dve, xt_done, b.n - 1)
                    xb = X[:, bass.ds(b.n * GT, GT), :]
                    normalise(lambda t: xb[:, t, :], lambda t: XN[:, b.r, t, :], b, sd_done, rstd_done, xn_done)
                if not whole and s.n < 2:
                    return
                b = s.back(2)
                dve.wait_ge(v_done, b.n + 1)
                nc.vector.tensor_copy(V[:, bass.ds(b.n * GW, GW)], bank(6 + b.r)).then_inc(v_kept, 1)
            steps(dve, 0, NG + 2, 2, stage1, peel=4, tail=2)

            def stage2(s):
                whole = not isinstance(s.n, int)
                if whole or s.n < NT:
                    sc = bank(2 * s.r, 2).rearrange("p (h k) -> p h k", h=H)
                    need(dve, sub_done, s.n - 1)
                    dve.wait_ge(s_done, s.n + 1)
                    nc.vector.tensor_reduce(MX[:, s.r, :], sc, axis=AX.X, op=ALU.max).then_inc(mx_done, 1)
                    dve.wait_ge(mx_done, s.n + 1)
                    need(dve, pt_done, s.n - 1)
                    nc.vector.tensor_tensor(SB[:, s.r].rearrange("p (h k) -> p h k", h=H), sc,
                                            MX[:, s.r, :].unsqueeze(2).to_broadcast([P, H, SEQ]), ALU.subtract).then_inc(sub_done, 1)
                if whole or s.n >= 3:
                    b = s.back(3)
                    dve.wait_ge(wo_done, b.n + 1)
                    xt = X[:, bass.ds(b.n, 1), :].rearrange("p a d -> p (a d)")
                    nc.vector.tensor_tensor(xt, bank(6 + b.r)[:, 256:384], xt, ALU.add).then_inc(x1_done, 1)
                if whole or 2 <= s.n < NT + 2:
                    b = s.back(2)
                    need(dve, ot_ready, b.n)
                    dve.wait_ge(od_done, b.n + 1)
                    nc.vector.reciprocal(RD[:], bank(6 + b.r)[:, 128:256]).then_inc(rd_done, 1)
                    dve.wait_ge(rd_done, b.n + 1)
                    need(dve, wo_done, b.n - 1)
                    nc.vector.tensor_tensor(OT[:, b.r, :], bank(6 + b.r)[:, 0:128], RD[:], ALU.mult).then_inc(ot_ready, 1)
            dve.wait_ge(xb_done, NG)
            steps(dve, 0, NT + 3, 2, stage2, peel=4, tail=3)

            for r in range(KR):
                dve.wait_ge(qs_in[r], 16 * (NT // KR))
            dve.wait_ge(vp_done, NT)
            dve.wait_ge(x1_done, NT)
            nc.vector.tensor_copy(BASE[:, 0, :], C[:, C_BASE:C_BASE + E]).then_inc(base_carry, 1)

            def stage3(s):
                whole = not isinstance(s.n, int)
                if whole or s.n < NG:
                    xg = X[:, bass.ds(s.n * GT, GT), :]
                    moments(lambda t: xg[:, t, :], s, stat2, half2, gap2, mv2, xn2)
                if whole or 1 <= s.n < NG + 1:
                    b = s.back(1)
                    need(dve, routed[b.r], 16 * GT * b.it)
                    xb = X[:, bass.ds(b.n * GT, GT), :]
                    normalise(lambda t: xb[:, t, :], lambda t: RG[:, b.r, t, 0:D], b, sd2, rstd2, xn2)
                if not whole and s.n < 2:
                    return
                b = s.back(2)
                bank_b = bank(2 + b.r)
                need(dve, dest_done, b.n)
                need(dve, desti_done, b.n)
                dve.wait_ge(lg_done, b.n + 1)
                nc.vector.tensor_tensor(LG[:], bank_b[:, 0:GT * E].rearrange("p (t e) -> p t e", e=E),
                                        BR[:].unsqueeze(1).to_broadcast([P, GT, E]), ALU.add).then_inc(lg_ready, 1)
                dve.wait_ge(lg_ready, b.n + 1)
                nc.vector.tensor_reduce(TOP[:], LG[:], axis=AX.X, op=ALU.max).then_inc(top_done, 1)
                dve.wait_ge(top_done, b.n + 1)
                nc.vector.tensor_tensor(PREF[:], LG[:], TOP[:].unsqueeze(2).to_broadcast([P, GT, E]), ALU.is_ge).then_inc(eq_done, 1)
                dve.wait_ge(eq_done, b.n + 1)
                nc.vector.tensor_tensor(LG[:], PREF[:], C[:, C_PREF:C_PREF + E].unsqueeze(1).to_broadcast([P, GT, E]), ALU.mult).then_inc(pref_done, 1)
                dve.wait_ge(pref_done, b.n + 1)
                nc.vector.tensor_reduce(TOP[:], LG[:], axis=AX.X, op=ALU.max).then_inc(best_done, 1)
                dve.wait_ge(best_done, b.n + 1)
                need(dve, rank_done, b.n - 1)
                nc.vector.tensor_tensor(HOT[:, b.r], LG[:], TOP[:].unsqueeze(2).to_broadcast([P, GT, E]), ALU.is_ge).then_inc(hot_done, 1)
                dve.wait_ge(hot_done, b.n + 1)
                dve.wait_ge(rank_done, b.n + 1)
                dve.wait_ge(base_carry, b.n + 1)
                bk = bank(4 + b.r)
                for t in range(GT):
                    nc.vector.tensor_tensor(BASE[:, t + 1, :], BASE[:, t, :], bk[:, 32 + t * E:32 + t * E + E], ALU.add).then_inc(base_step, 1)
                    dve.wait_ge(base_step, b.n * GT + t + 1)
                nc.vector.tensor_tensor(POS[:], bk[:, 0:32].rearrange("p (t e) -> p t e", e=E), BASE[:, 0:GT, :], ALU.add).then_inc(pos_done, 1)
                dve.wait_ge(pos_done, b.n + 1)
                nc.vector.tensor_copy(BASE[:, 0, :], BASE[:, GT, :]).then_inc(base_carry, 1)
                nc.vector.tensor_tensor(LG[:], POS[:], HOT[:, b.r], ALU.mult).then_inc(posm_done, 1)
                dve.wait_ge(posm_done, b.n + 1)
                nc.vector.tensor_reduce(DEST[:], LG[:], axis=AX.X, op=ALU.add).then_inc(dest_done, 1)
                dve.wait_ge(dest_done, b.n + 1)
                need(dve, routed[b.r], 16 * GT * b.it)
                nc.vector.tensor_copy(DESTI[:, b.r, :], DEST[:]).then_inc(desti_done, 1)
            steps(dve, 0, NG + 2, 2, stage3, peel=4, tail=2)

            dve.wait_ge(base_carry, NG + 1)
            nc.vector.tensor_copy(CNTI[:], BASE[0:1, 0, :]).then_inc(cnt_ready, 1)
            made = [0]

            def link(ins):
                made[0] += 1
                ins.then_inc(tab_step, 1)
                dve.wait_ge(tab_step, made[0])

            def row(k):
                return TE[0:1, k, :]
            link(nc.vector.tensor_tensor(row(0), BASE[0:1, 0, :], C[0:1, C_BASE:C_BASE + E], ALU.subtract))
            cm = CMP[0:1, 0:E * NT].rearrange("p (e m) -> p e m", e=E)
            link(nc.vector.tensor_tensor(cm, row(0).unsqueeze(2).to_broadcast([1, E, NT]),
                                         C[0:1, C_LIM:C_LIM + NT].unsqueeze(1).to_broadcast([1, E, NT]), ALU.is_gt))
            link(nc.vector.tensor_reduce(row(1), cm, axis=AX.X, op=ALU.add))
            src, dst = 1, 2
            for d in (1, 2, 4):
                link(nc.vector.tensor_copy(TE[0:1, dst, 0:d], TE[0:1, src, 0:d]))
                link(nc.vector.tensor_tensor(TE[0:1, dst, d:E], TE[0:1, src, d:E], TE[0:1, src, 0:E - d], ALU.add))
                src, dst = dst, dst + 1
            past = CMP[0:1, :].rearrange("p (i e) -> p i e", e=E)
            link(nc.vector.tensor_tensor(past, C[0:1, C_BLK:C_BLK + NB].unsqueeze(2).to_broadcast([1, NB, E]),
                                         row(src).unsqueeze(1).to_broadcast([1, NB, E]), ALU.is_ge))
            link(nc.vector.tensor_reduce(TB[0:1, 0, :], past, axis=AX.X, op=ALU.add))
            link(nc.vector.tensor_tensor(past, past, row(1).unsqueeze(1).to_broadcast([1, NB, E]), ALU.mult))
            link(nc.vector.tensor_reduce(TB[0:1, 1, :], past, axis=AX.X, op=ALU.add))
            link(nc.vector.tensor_tensor(TB[0:1, 2, :], C[0:1, C_BLK:C_BLK + NB], TB[0:1, 1, :], ALU.subtract))
            link(nc.vector.tensor_scalar(TB[0:1, 1, :], TB[0:1, 0, :], float(CAP), None, ALU.mult))
            link(nc.vector.scalar_tensor_tensor(TB[0:1, 3, :], TB[0:1, 2, :], float(P), TB[0:1, 1, :], ALU.mult, ALU.add))
            link(nc.vector.tensor_copy(TABI[:, 0, :], TB[0:1, 3, :]))
            link(nc.vector.tensor_scalar(TB[0:1, 2, :], TB[0:1, 0, :], float(E - 1), None, ALU.min))
            nc.vector.tensor_copy(TABI[:, 1, :], TB[0:1, 2, :]).then_inc(tab_ready, 1)

            dve.wait_ge(w2_in, 48)
            dve.wait_ge(tab_ready, 1)
            def ffn(s):
                whole = not isinstance(s.n, int)
                if whole or s.n < NB:
                    ex = dve.value_load(TABI[0:1, 1, bass.ds(s.n, 1)], min_val=0, max_val=E - 1)
                    dve.wait_ge(h_done, s.n + 1)
                    need(dve, y_done, s.n - 1)
                    nc.vector.tensor_tensor(HT[:, s.r % 2, :].rearrange("p (c t) -> p c t", c=FC),
                                            bank(2 + s.r % 2).rearrange("p (c t) -> p c t", c=FC),
                                            B1[:, bass.ds(ex, 1), :].rearrange("p a c -> p (a c)").unsqueeze(2).to_broadcast([P, FC, P]),
                                            ALU.add).then_inc(hb_done, 1)
                if whole or s.n >= 1:
                    b = s.back(1)
                    exb = dve.value_load(TABI[0:1, 1, bass.ds(b.n, 1)], min_val=0, max_val=E - 1)
                    need(dve, y_out[b.r], 16 * b.it)
                    dve.wait_ge(y_done, b.n + 1)
                    nc.vector.tensor_tensor(YO[:, b.r, :], bank(4 + b.r % 2)[:, 0:D],
                                            B2[:, bass.ds(exb, 1), :].rearrange("p a c -> p (a c)"), ALU.add).then_inc(yx_done, 1)
                    dve.wait_ge(yx_done, b.n + 1)
                    nc.vector.tensor_tensor(YO[:, b.r, :], YO[:, b.r, :], RT[:, b.r, D:2 * D], ALU.add).then_inc(yo_ready, 1)
            steps(dve, 0, NB + 1, 4, ffn, peel=4, tail=1)

        @block.tensor
        def _(pe):
            pe.wait_ge(con_in, 16 * 12)
            nc.tensor.matmul(bank(0)[:, 0:D], BV[:], WO[:], start=True, stop=True).then_inc(bo_mm, 1)
            pe.wait_ge(bo_ready, 1)

            def stage1(s):
                whole = not isinstance(s.n, int)
                pe.wait_ge(xn_done, s.n + 1)
                need(pe, xnt_ready, s.n - 1)
                for t in range(GT):
                    last = nc.tensor.transpose(bank(s.r)[:, t * P:(t + 1) * P], XN[:, s.r, t, :], ident)
                last.then_inc(xt_done, 1)
                pe.wait_ge(ct_in[s.r], 16 * (s.it + 1))
                need(pe, k_kept, s.n - 1)
                nc.tensor.matmul(bank(4 + s.r), WK[:], CT[:, s.r, :], start=True, stop=True).then_inc(k_done, 1)
                need(pe, v_kept, s.n - 1)
                for b in range(2 * GT):
                    for r in range(2):
                        h = slice(SEQ * r, SEQ * r + SEQ)
                        last = nc.tensor.matmul(bank(6 + s.r)[h, b * SEQ:(b + 1) * SEQ], CT[:, s.r, b * SEQ:(b + 1) * SEQ],
                                                WV[:, h], start=True, stop=True)
                last.then_inc(v_done, 1)
                pe.wait_ge(xnt_ready, s.n + 1)
                need(pe, q_kept, s.n - 1)
                nc.tensor.matmul(bank(2 + s.r), WQ[:], XNT[:, s.r, :], start=True, stop=True).then_inc(q_done, 1)
            steps(pe, 0, NG, 2, stage1, peel=2)

            pe.wait_ge(q_kept, NG)
            pe.wait_ge(v_kept, NG)
            ob = C[:, C_OB:C_OB + 64].rearrange("p (s m) -> p s m", s=2)

            def stage2(s):
                whole = not isinstance(s.n, int)
                if whole or s.n < NT:
                    pe.wait_ge(qs_in[s.r], 16 * (s.it + 1))
                    pe.wait_ge(km_in[s.r], 64 * (s.it + 1))
                    need(pe, sub_done, s.n - 1)
                    for half in range(2):
                        for b in range(2):
                            q = QS[:, s.r, SEQ * b:SEQ * b + SEQ]
                            k = KM[:, s.r, b, 8 * half:8 * half + 8, :]
                            last = nc.tensor.matmul(bank(2 * (s.r % 2) + half)[SEQ * b:SEQ * b + SEQ, :], q, k, start=True, stop=True)
                    last.then_inc(s_done, 1)
                if whole or s.n >= 3:
                    b3 = s.back(3)
                    pe.wait_ge(ot_ready, b3.n + 1)
                    nc.tensor.matmul(bank(6 + b3.r % 2)[:, 256:384], OT[:, b3.r % 2, :], WO[:], start=True, stop=True).then_inc(wo_done, 1)
                if whole or 1 <= s.n < NT + 1:
                    b1 = s.back(1)
                    pe.wait_ge(exp_done, b1.n + 1)
                    need(pe, pt_ready, b1.n)
                    for hp in range(HP):
                        last = nc.tensor.transpose(bank(4, 2)[:, hp * P:(hp + 1) * P], SB[:, b1.r % 2, hp * P:(hp + 1) * P], ident)
                    last.then_inc(pt_done, 1)
                if whole or 2 <= s.n < NT + 2:
                    b2 = s.back(2)
                    pe.wait_ge(pt_ready, b2.n + 1)
                    pe.wait_ge(vp_done, b2.n + 1)
                    need(pe, x1_done, b2.n - 1)
                    for b in range(2):
                        for z in range(2):
                            for c in range(4):
                                nc.tensor.matmul(bank(6 + b2.r % 2)[32 * c:32 * c + 32, SEQ * b:SEQ * b + SEQ],
                                                 VP[:, b2.r % 2, b, 2 * c + z, :], PT[:, b2.r % 2, 2 * c + z, SEQ * b:SEQ * b + SEQ],
                                                 start=z == 0, stop=z == 1)
                    for z in range(2):
                        for c in range(4):
                            last = nc.tensor.matmul(bank(6 + b2.r % 2)[32 * c:32 * c + 32, P:2 * P], ob[:, z, :],
                                                    PT[:, b2.r % 2, 2 * c + z, :], start=z == 0, stop=z == 1)
                    last.then_inc(od_done, 1)
            steps(pe, 0, NT + 3, KR, stage2, peel=4, tail=3)

            pe.wait_ge(sub_done, NT)
            pe.wait_ge(x1_done, NT)
            pe.wait_ge(pt_ready, NT)
            def stage3(s):
                whole = not isinstance(s.n, int)
                if whole or s.n < NG:
                    pe.wait_ge(xn2, s.n + 1)
                    need(pe, x1t_ready, s.n - 1)
                    for t in range(GT):
                        last = nc.tensor.transpose(bank(s.r)[:, t * P:(t + 1) * P], RG[:, s.r, t, 0:D], ident)
                    last.then_inc(xt2_done, 1)
                if whole or s.n >= 1:
                    b = s.back(1)
                    pe.wait_ge(hot_done, b.n + 1)
                    need(pe, pos_done, b.n - 1)
                    hot = HOT[:, b.r].rearrange("p t e -> p (t e)")
                    nc.tensor.matmul(bank(4 + b.r)[:, 0:32], tri, hot, start=True, stop=True)
                    nc.tensor.matmul(bank(4 + b.r)[:, 32:64], ones, hot, start=True, stop=True).then_inc(rank_done, 1)
                if whole or s.n < NG:
                    pe.wait_ge(x1t_ready, s.n + 1)
                    need(pe, lg_ready, s.n - 1)
                    for t in range(GT):
                        last = nc.tensor.matmul(bank(2 + s.r)[:, t * E:(t + 1) * E], X1T[:, s.r, t * P:(t + 1) * P], WR[:], start=True, stop=True)
                    last.then_inc(lg_done, 1)
            steps(pe, 0, NG + 1, 2, stage3, peel=4, tail=1)

            pe.wait_ge(w2_in, 48)
            pe.wait_ge(tab_ready, 1)
            def transpose_rows(s):
                whole = not isinstance(s.n, int)
                pe.wait_ge(rt_in[s.r], 16 * (s.it + 1))
                need(pe, bxt_ready, s.n - 1)
                nc.tensor.transpose(bank(s.r % 2)[:, 0:P], RT[:, s.r, 0:D], ident).then_inc(bx_done, 1)

            def ffn(s):
                whole = not isinstance(s.n, int)
                if whole or s.n < NB:
                    transpose_rows(s)
                if whole or 1 <= s.n < NB + 1:
                    b = s.back(1)
                    pe.wait_ge(bxt_ready, b.n + 1)
                    pe.wait_ge(w1_in[b.r], 16 * (b.it + 1))
                    need(pe, hb_done, b.n - 1)
                    for c in range(FC):
                        last = nc.tensor.matmul(bank(2 + b.r % 2)[:, c * P:(c + 1) * P], W1[:, b.r, c * P:(c + 1) * P],
                                                XT[:, b.r % 2, :], start=True, stop=True)
                    last.then_inc(h_done, 1)
                if whole or s.n >= 2:
                    b = s.back(2)
                    ex = pe.value_load(TABI[0:1, 1, bass.ds(b.n, 1)], min_val=0, max_val=E - 1)
                    pe.wait_ge(h_ready, b.n + 1)
                    need(pe, yx_done, b.n - 1)
                    for c in range(FC):
                        w = W2[:, bass.ds(ex, 1), c, :].rearrange("p a d -> p (a d)")
                        last = nc.tensor.matmul(bank(4 + b.r % 2)[:, 0:D], HT[:, b.r % 2, c * P:(c + 1) * P], w,
                                                start=c == 0, stop=c == FC - 1)
                    last.then_inc(y_done, 1)
            steps(pe, 0, NB + 2, 4, ffn, peel=4, tail=2)


def kernel(x, ctx_1024, L0_xattn_Wq, L0_xattn_bq, L0_xattn_Wk, L0_xattn_bk, L0_xattn_Wv, L0_xattn_bv,
           L0_xattn_Wo, L0_xattn_bo, L0_ffn_Wr, L0_ffn_br, L0_ffn_W1, L0_ffn_b1, L0_ffn_W2, L0_ffn_b2):
    import concourse.bacc as bacc
    from concourse.bass_utils import run_bass_kernel_spmd

    def lay(a):
        return np.ascontiguousarray(a)

    con, pad, ids = constants()
    n = np.asarray
    arrays = {
        "x": lay(n(x).reshape(TOK, D)),
        "ctxT": lay(n(ctx_1024).reshape(TOK, D).T),
        "wq": lay(n(L0_xattn_Wq).T), "wk": lay(n(L0_xattn_Wk).T),
        "wv": lay(n(L0_xattn_Wv).reshape(HP, 2, DK, D).transpose(3, 1, 0, 2).reshape(D, D)), "wo": lay(n(L0_xattn_Wo).T),
        "bq": lay(n(L0_xattn_bq).reshape(D, 1)), "bk": lay(n(L0_xattn_bk).reshape(D, 1)),
        "bv": lay(np.broadcast_to(n(L0_xattn_bv)[:, None], (D, P))),
        "bo": lay(np.broadcast_to(n(L0_xattn_bo)[None], (P, D))),
        "wr": lay(n(L0_ffn_Wr).T), "br": lay(np.broadcast_to(n(L0_ffn_br)[None], (P, E))),
        "w1": lay(n(L0_ffn_W1).transpose(2, 0, 1).reshape(D, E * F)),
        "b1": lay(n(L0_ffn_b1).reshape(E, FC, P).transpose(2, 0, 1)),
        "w2": lay(n(L0_ffn_W2).reshape(E, D, FC, P).transpose(3, 0, 2, 1)),
        "b2": lay(np.broadcast_to(n(L0_ffn_b2)[None], (P, E, D))),
        "con": con, "pad": pad, "ids": ids,
    }
    nc = bacc.Bacc("TRN2", target_bir_lowering=False, num_devices=1)
    args = [nc.dram_tensor("in_" + k, a.shape, mybir.dt.from_np(a.dtype), kind="ExternalInput").ap()
            for k, a in arrays.items()]
    out = nc.dram_tensor("out", (TOK, D), mybir.dt.float32, kind="ExternalOutput").ap()
    build(nc, *args, out)
    r = run_bass_kernel_spmd(nc, [{"in_" + k: a for k, a in arrays.items()}], core_ids=[0])
    return r.results[0]["out"].reshape(BATCH, SEQ, D)
```

```python
import concourse.bass as bass
from concourse import mybir
from contextlib import ExitStack
import numpy as np

P = 128
D = 128
SEQ = 64
BATCH = 128
TOK = BATCH * SEQ
NT = TOK // P
GT = 4
NG = NT // GT
GW = GT * P
H = 16
DK = D // H
HP = H // 2
E = 8
F = 512
FC = F // P
CAP = TOK + P
NB = TOK // P + E
PADS = NB - TOK // P
ROWS = E * CAP + PADS * P
KR = 4
ST = 4 * GT
NS = NT // ST
RR = 8
RW = 2 * D + 4
ID = 2 * D
EPS = 1e-5
SCALE = float(1.0 / np.sqrt(np.float32(DK)))

C_ID, C_TRI, C_ONE, C_OB, C_JM, C_PREF, C_BASE, C_LIM, C_BLK, C_EPS, C_END = np.cumsum(
    [0, P, P, P, 2 * 32, 4 * SEQ, E, E, NT, NB, 1]).tolist()


def constants():
    c = np.zeros((P, C_END), np.float32)
    p = np.arange(P)
    c[:, C_ID:C_ID + P] = np.eye(P)
    c[:, C_TRI:C_TRI + P] = p[:, None] < p[None, :]
    c[:, C_ONE:C_ONE + P] = 1
    for s in range(2):
        for r in range(2):
            a = C_OB + 32 * s + 16 * s + DK * r
            c[SEQ * r:SEQ * r + SEQ, a:a + DK] = 1
    for j in range(4):
        c[(p // DK) % 4 == j, C_JM + SEQ * j:C_JM + SEQ * (j + 1)] = 1
    c[:, C_PREF:C_PREF + E] = E - np.arange(E)
    c[:, C_BASE:C_BASE + E] = CAP * np.arange(E)
    c[:, C_LIM:C_LIM + NT] = P * np.arange(NT)
    c[:, C_BLK:C_BLK + NB] = np.arange(NB)
    c[:, C_EPS] = EPS
    pad = np.zeros((P, RW), np.float32)
    pad[:, ID] = np.full(P, TOK, np.int32).view(np.float32)
    ids = np.ascontiguousarray(np.arange(TOK, dtype=np.int32).reshape(NT, P).T)
    return c, pad, ids


class Step:

    def __init__(self, it, r, ring):
        self.it, self.r, self.ring = it, r, ring
        self.n = it * ring + r

    def back(self, k):
        q, r = divmod(self.r - k, self.ring)
        return Step(self.it + q if q else self.it, r, self.ring)


def need(eng, sem, value):
    if not isinstance(value, int) or value > 0:
        eng.wait_ge(sem, value)


def steps(eng, first, last, ring, body, peel=0, tail=0):
    lo = -(-max(first, peel) // ring)
    hi = (last - tail) // ring
    for n in range(first, lo * ring):
        body(Step(n // ring, n % ring, ring))
    if hi - lo > 1:
        with eng.Fori(lo, hi) as it:
            for r in range(ring):
                body(Step(it, r, ring))
    else:
        hi = lo
    for n in range(hi * ring, last):
        body(Step(n // ring, n % ring, ring))


def build(nc, x, ctxT, wq, wk, wv, wo, bq, bk, bv, bo, wr, br, w1, b1, w2, b2, con, pad, ids, out):
    f32, i32 = mybir.dt.float32, mybir.dt.int32
    ALU, ACT, AX = mybir.AluOpType, mybir.ActivationFunctionType, mybir.AxisListType
    x_v = x.rearrange("(t p) d -> p t d", p=P)
    rows = nc.dram_tensor("rows", (ROWS, RW), f32).ap()

    ctx = ExitStack()
    with ctx:
        def sb(name, *shape, dt=f32):
            return ctx.enter_context(nc.sbuf_tensor(name, list(shape), dt))

        def sem(name):
            return ctx.enter_context(nc.semaphore(name))

        def sems(name, n):
            return [sem(f"{name}{i}") for i in range(n)]

        X = sb("X", P, NT, D)
        BIG = sb("BIG", P, 3 * TOK)
        QT = BIG[:, 0:TOK]
        KT = BIG[:, TOK:2 * TOK]
        V = BIG[:, 2 * TOK:3 * TOK]
        C = sb("C", P, C_END)
        ident, tri, ones = C[:, C_ID:C_ID + P], C[:, C_TRI:C_TRI + P], C[:, C_ONE:C_ONE + P]
        WQ, WK, WV, WO = (sb(n, P, D) for n in ("WQ", "WK", "WV", "WO"))
        BV, BO = sb("BV", P, D), sb("BO", P, D)
        BQK = sb("BQK", P, 2)
        WR, BR = sb("WR", P, E), sb("BR", P, E)
        STAT = sb("STAT", P, GT, 6)
        MS = sb("MS", P, 4, GT)
        MV = sb("MV", P, 2, 2, GT)
        SD = sb("SD", P, 2, GT)
        RSTD = sb("RSTD", P, GT)
        QS = sb("QS", P, KR, P)
        KJ = sb("KJ", P, KR, 2, 4, SEQ)
        KM = sb("KM", P, KR, 2, H, SEQ)
        SB = sb("SB", P, 2, H * SEQ)
        MX = sb("MX", P, 2, H)
        PT = sb("PT", P, 2, HP, P)
        XN = SB[:].rearrange("p r (t d) -> p (r t) d", d=D)[:, 0:2 * GT, :].rearrange("p (r t) d -> p r t d", r=2)
        XNT = SB[:, 1, :].rearrange("p (r w) -> p r w", r=2)
        CT = PT[:, 0].rearrange("p (r a) d -> p r (a d)", r=2)
        VP = sb("VP", P, 2, 2, HP, 32)
        RD = sb("RD", P, P)
        OT = sb("OT", P, 2, P)

        def big(at, *shape):
            n = int(np.prod(shape))
            v = BIG[:, at:at + n]
            if len(shape) == 2:
                v = v.rearrange("p (a b) -> p a b", a=shape[0])
            if len(shape) == 3:
                v = v.rearrange("p (a b c) -> p a b c", a=shape[0], b=shape[1])
            return v, at + n

        at = 0
        RG, at = big(at, NT, RW)
        X1T, at = big(at, ST * P)
        STAT2, at = big(at, ST, 6)
        MS2, at = big(at, 4, ST)
        MV2, at = big(at, 1, 2, ST)
        SD2, at = big(at, 1, ST)
        RSTD2, at = big(at, ST)
        LG, at = big(at, ST, E)
        TOP, at = big(at, ST)
        HOT, at = big(at, ST + 1, E)
        PREF, at = big(at, ST, E)
        BASE, at = big(at, E)
        POS, at = big(at, ST + 1, E)
        DEST, at = big(at, ST)
        PADR, at = big(at, RW)
        CMP, at = big(at, NB * E)
        TE, at = big(at, 6, E)
        TB, at = big(at, 4, NB)
        B1, at = big(at, E, FC)
        B2, at = big(at, E, D)
        RT, at = big(at, RR, RW)
        XT, at = big(at, 2, P)
        km = KM[:].rearrange("p r b h k -> p (r b h k)")
        W2 = km[:, E * F:2 * E * F].rearrange("p (e c d) -> p e c d", e=E, c=FC)
        HT = SB[:, 0, :].rearrange("p (r f) -> p r f", r=2)
        YO = SB[:, 1, :].rearrange("p (r d) -> p r d", r=RR)
        W1S = PT[:].rearrange("p r a b -> p (r a b)").rearrange("p (r f) -> p r f", r=4)
        assert at <= 3 * TOK
        IDS = sb("IDS", P, NT, dt=i32)
        DESTI = sb("DESTI", P, NS, ST, dt=i32)
        TABI = sb("TABI", 1, 2, NB, dt=i32)
        CNTI = sb("CNTI", 1, E, dt=i32)

        PS = ctx.enter_context(nc.psum_tensor("PS", [P, 8 * 512], f32))

        def bank(k, n=1):
            return PS[:, 512 * k:512 * (k + n)]

        con_in, con2_in, w2_in = sem("con_in"), sem("con2_in"), sem("w2_in")
        x_in, ct_in = sems("x_in", 2), sems("ct_in", 2)
        stat_done, mv_done, sd_done, rstd_done, xn_done = (sem(n) for n in ("stat_done", "mv_done", "sd_done", "rstd_done", "xn_done"))
        xt_done, xnt_ready = sem("xt_done"), sem("xnt_ready")
        q_done, k_done, v_done = sem("q_done"), sem("k_done"), sem("v_done")
        q_kept, k_kept, v_kept = sem("q_kept"), sem("k_kept"), sem("v_kept")
        bo_mm, bo_ready, xb_done = sem("bo_mm"), sem("bo_ready"), sem("xb_done")
        zeroed = sem("zeroed")
        qs_in, km_in = sems("qs_in", KR), sems("km_in", KR)
        kj_done, vp_done = sem("kj_done"), sem("vp_done")
        s_done, mx_done, sub_done, exp_done = (sem(n) for n in ("s_done", "mx_done", "sub_done", "exp_done"))
        pt_done, pt_ready, od_done, rd_done, ot_ready = (sem(n) for n in ("pt_done", "pt_ready", "od_done", "rd_done", "ot_ready"))
        wo_done, x1_done = sem("wo_done"), sem("x1_done")
        half_done, gap_done, half2, gap2 = (sem(n) for n in ("half_done", "gap_done", "half2", "gap2"))
        stat2, mv2, sd2, rstd2, xn2 = (sem(n) for n in ("stat2", "mv2", "sd2", "rstd2", "xn2"))
        x1c_done, id_done, xt2_done, x1t_ready = (sem(n) for n in ("x1c_done", "id_done", "xt2_done", "x1t_ready"))
        lg_done, lg_ready, top_done, eq_done, pref_done, best_done, hot_done = (
            sem(n) for n in ("lg_done", "lg_ready", "top_done", "eq_done", "pref_done", "best_done", "hot_done"))
        rank_done, base_first, pos_done, posm_done, dest_done, desti_done = (
            sem(n) for n in ("rank_done", "base_step", "pos_done", "posm_done", "dest_done", "desti_done"))
        base_carry = sem("base_carry")
        routed, sent = sem("routed"), sem("sent")
        padr_in, pads_out, pad_out = sem("padr_in"), sem("pads_out"), sem("pad_out")
        cnt_ready, tab_step, tab_ready = sem("cnt_ready"), sem("tab_step"), sem("tab_ready")
        rt_in, w1_in, y_out = sems("rt_in", RR), sems("w1_in", 4), sems("y_out", RR)
        w1_all = sem("w1_all")
        bx_done, bxt_ready, h_done, hb_done, h_ready = (sem(n) for n in ("bx_done", "bxt_ready", "h_done", "hb_done", "h_ready"))
        y_done, yx_done, yo_ready = sem("y_done"), sem("yx_done"), sem("yo_ready")

        block = ctx.enter_context(nc.Block())

        @block.sync
        def _(sp):
            for dst, src in ((C[:], con), (WQ[:], wq), (WK[:], wk), (WV[:], wv), (BQK[:, 0:1], bq),
                             (BQK[:, 1:2], bk), (WO[:], wo), (BV[:], bv), (BO[:], bo), (WR[:], wr),
                             (BR[:], br), (IDS[:], ids)):
                sp.dma_start(dst, src).then_inc(con_in, 16)

            def load_group(s):
                def go(before):
                    if before:
                        sp.wait_ge(stat_done, s.n - 1)
                    sp.dma_start(X[:, bass.ds(s.n * GT, GT), :], x_v[:, bass.ds(s.n * GT, GT), :]).then_inc(x_in[s.r], 16)
                    if before:
                        sp.wait_ge(v_done, s.n - 1)
                        sp.wait_ge(k_done, s.n - 1)
                    sp.dma_start(CT[:, s.r, :], ctxT[:, bass.ds(s.n * GW, GW)]).then_inc(ct_in[s.r], 16)
                go(not isinstance(s.n, int) or s.n >= 2)
            steps(sp, 0, NG, 2, load_group, peel=2)

            sp.wait_ge(q_kept, NG)
            sp.wait_ge(zeroed, 2)
            def spread(s):
                need(sp, s_done, s.n - KR + 1)
                sp.dma_start(QS[:, s.r, :], QT[:, bass.ds(s.n * P, P)]).then_inc(qs_in[s.r], 16)
                sp.wait_ge(kj_done, s.n + 1)
                for g in range(4):
                    r = slice(32 * g, 32 * g + 32)
                    sp.dma_start(KM[r, s.r, :, 4 * g:4 * g + 4, :], KJ[r, s.r]).then_inc(km_in[s.r], 16)
            steps(sp, 0, NT, KR, spread, peel=4)

            sp.wait_ge(s_done, NT)
            sp.dma_start(km[:, 0:E * F], w1).then_inc(w1_all, 16)
            sp.dma_start(W2, w2).then_inc(w2_in, 16)
            sp.wait_ge(vp_done, NT)
            for r in range(KR):
                sp.wait_ge(qs_in[r], 16 * (NT // KR))
            sp.dma_start(PADR[:], pad).then_inc(padr_in, 16)
            sp.dma_start(B1[:], b1).then_inc(w2_in, 16)
            sp.dma_start(B2[:], b2).then_inc(w2_in, 16)
            sp.wait_ge(padr_in, 16)
            for k in range(PADS):
                sp.dma_start(rows[E * CAP + k * P:E * CAP + (k + 1) * P, :], PADR[:]).then_inc(pads_out, 16)
            sp.wait_ge(cnt_ready, 1)
            for e in range(E // 2):
                end = sp.value_load(CNTI[0:1, e:e + 1], min_val=0, max_val=ROWS - P)
                sp.dma_start(rows[bass.ds(end, P), :], PADR[:]).then_inc(pads_out, 16)

            sp.wait_ge(tab_ready, 1)
            sp.wait_ge(w1_all, 16)
            sp.wait_ge(pads_out, 16 * (PADS + E))
            sp.wait_ge(routed, 16 * NT)
            def load_block(s):
                whole = not isinstance(s.n, int)
                if whole or s.n < NB:
                    row = sp.value_load(TABI[0:1, 0, bass.ds(s.n, 1)], min_val=0, max_val=ROWS - P)
                    need(sp, y_out[s.r], 16 * s.it)
                    sp.dma_start(RT[:, s.r, :], rows[bass.ds(row, P), :]).then_inc(rt_in[s.r], 16)
                if whole or s.n >= 3:
                    b = s.back(3)
                    ex = sp.value_load(TABI[0:1, 1, bass.ds(b.n, 1)], min_val=0, max_val=E - 1)
                    need(sp, h_done, b.n - 3)
                    sp.dma_start(W1S[:, b.r % 4, :], km[:, bass.ds(ex * F, F)]).then_inc(w1_in[b.r % 4], 16)
            steps(sp, 0, NB + 3, RR, load_block, peel=RR, tail=3)

        @block.gpsimd
        def _(pool):
            nc.gpsimd.memset(KM[:], 0.0).then_inc(zeroed, 1)
            nc.gpsimd.memset(VP[:], 0.0).then_inc(zeroed, 1)

            pool.wait_ge(bo_ready, 1)
            def add_bias(s):
                pool.wait_ge(xn_done, s.n + 1)
                g = X[:, bass.ds(s.n * GT, GT), :]
                nc.gpsimd.tensor_tensor(g, g, BO[:].unsqueeze(1).to_broadcast([P, GT, D]), ALU.add).then_inc(xb_done, 1)
            steps(pool, 0, NG, 2, add_bias)

            jmask = C[:, C_JM:C_JM + 4 * SEQ].rearrange("p (j k) -> p j k", j=4)
            pool.wait_ge(k_kept, NG)
            pool.wait_ge(v_kept, NG)
            pool.wait_ge(zeroed, 2)
            def masks(s):
                whole = not isinstance(s.n, int)
                if whole or s.n < NT:
                    need(pool, km_in[s.r], 64 * s.it)
                    for b in range(2):
                        k = KT[:, bass.ds(s.n * P + SEQ * b, SEQ)].unsqueeze(1).to_broadcast([P, 4, SEQ])
                        last = nc.gpsimd.tensor_tensor(KJ[:, s.r, b], k, jmask, ALU.mult)
                    last.then_inc(kj_done, 1)
                if whole or s.n >= 3:
                    t = s.back(3)
                    need(pool, od_done, t.n - 1)
                    for z in range(2):
                        dst = VP[:, t.r % 2].rearrange("p b (c z) m -> p (b c) z m", z=2)[:, :, z, 16 * z:16 * z + 16].rearrange("p g (r w) -> p g r w", w=DK)
                        v = V[:, bass.ds(t.n * P, P)].rearrange("p (g z w) -> p g z w", z=2, w=DK)[:, :, z, :].unsqueeze(2).to_broadcast([P, 8, 2, DK])
                        own = C[:, C_OB:C_OB + 16].rearrange("p (r w) -> p r w", w=DK).unsqueeze(1).to_broadcast([P, 8, 2, DK])
                        last = nc.gpsimd.tensor_tensor(dst, v, own, ALU.mult)
                    last.then_inc(vp_done, 1)
            steps(pool, 0, NT + 3, KR, masks, peel=8, tail=3)

            last_row, last_token = pool.to_reg(ROWS - 1), pool.to_reg(TOK - 1)
            pool.wait_ge(x1_done, NT)
            for r in range(KR):
                pool.wait_ge(qs_in[r], 16 * (NT // KR))
            nc.gpsimd.tensor_copy(RG[:, :, ID:ID + 1].bitcast(i32), IDS[:].unsqueeze(2)).then_inc(id_done, 1)
            pool.wait_ge(id_done, 1)

            def route(s):
                pool.wait_ge(dest_done, s.n + 1)
                nc.gpsimd.tensor_copy(DESTI[:, s.r, :], DEST[:]).then_inc(desti_done, 1)
                pool.wait_ge(desti_done, s.n + 1)
                pool.wait_ge(x1c_done, s.n + 1)
                pool.sem_inc(sent, 1)
                for t in range(ST):
                    at = s.n * ST + t
                    nc.gpsimd.indirect_dma_start(
                        out=rows, out_offset=bass.IndirectOffsetOnAxis(ap=DESTI[:, s.r, t:t + 1], axis=0),
                        in_=RG[:, bass.ds(at, 1), :].rearrange("p a w -> p (a w)"), in_offset=None,
                        bounds_check=last_row, oob_is_err=False).then_inc(routed, 16)
            steps(pool, 0, NS, NS, route)

            def home(s):
                pool.wait_ge(yo_ready, s.n + 1)
                pool.sem_inc(sent, 1)
                nc.gpsimd.indirect_dma_start(
                    out=out, out_offset=bass.IndirectOffsetOnAxis(ap=RT[:, s.r, ID:ID + 1].bitcast(i32), axis=0),
                    in_=YO[:, s.r, :], in_offset=None, bounds_check=last_token, oob_is_err=False).then_inc(y_out[s.r], 16)
            steps(pool, 0, NB, RR, home)
            for r in range(RR):
                pool.wait_ge(y_out[r], 16 * (NB // RR))

        @block.scalar
        def _(act):
            act.wait_ge(con_in, 16 * 12)

            def root(s, dst, src, mv, sd, rstd):
                need(act, rstd, s.n + 1 - s.ring)
                act.wait_ge(mv, s.n + 1)
                nc.scalar.activation(dst[:, s.r, :], src[:, s.r, 1, :], ACT.Sqrt, bias=C[:, C_EPS:C_EPS + 1]).then_inc(sd, 1)

            def keep(t):
                whole = not isinstance(t.n, int)
                if whole or t.n < NG:
                    root(t, SD, MV, mv_done, sd_done, rstd_done)
                if not whole and t.n < 1:
                    return
                s = t.back(1)
                act.wait_ge(xt_done, s.n + 1)
                need(act, q_done, s.n - 1)
                nc.scalar.copy(XNT[:, s.r, :], bank(s.r)).then_inc(xnt_ready, 1)
                act.wait_ge(k_done, s.n + 1)
                nc.scalar.activation(KT[:, bass.ds(s.n * GW, GW)], bank(4 + s.r), ACT.Identity, bias=BQK[:, 1:2]).then_inc(k_kept, 1)
                act.wait_ge(q_done, s.n + 1)
                nc.scalar.activation(QT[:, bass.ds(s.n * GW, GW)], bank(2 + s.r), ACT.Identity, bias=BQK[:, 0:1]).then_inc(q_kept, 1)
            steps(act, 0, NG + 1, 2, keep, peel=4, tail=1)

            def softmax(s):
                if isinstance(s.n, int) and s.n >= NT:
                    pass
                else:
                    act.wait_ge(sub_done, s.n + 1)
                    nc.scalar.activation(SB[:, s.r, :], SB[:, s.r, :], ACT.Exp, scale=SCALE).then_inc(exp_done, 1)
                if isinstance(s.n, int) and s.n < 1:
                    return
                b = s.back(1)
                act.wait_ge(pt_done, b.n + 1)
                need(act, od_done, b.n - 1)
                nc.scalar.copy(PT[:, b.r].rearrange("p a b -> p (a b)"), bank(4, 2)).then_inc(pt_ready, 1)
            steps(act, 0, NT + 1, 2, softmax, peel=4, tail=1)

            act.wait_ge(x1_done, NT)
            for r in range(KR):
                act.wait_ge(qs_in[r], 16 * (NT // KR))
            def stage3(s):
                root(s, SD2, MV2, mv2, sd2, rstd2)
                nc.scalar.copy(RG[:, bass.ds(s.n * ST, ST), D:2 * D], X[:, bass.ds(s.n * ST, ST), :]).then_inc(x1c_done, 1)
                need(act, lg_done, s.n)
                for j in range(4):
                    act.wait_ge(xt2_done, s.n * 4 + j + 1)
                    nc.scalar.copy(X1T[:, j * GW:(j + 1) * GW], bank(j)).then_inc(x1t_ready, 1)
            steps(act, 0, NS, 1, stage3, peel=1)

            def ffn(s):
                if not (isinstance(s.n, int) and s.n >= NB):
                    act.wait_ge(bx_done, s.n + 1)
                    need(act, h_done, s.n - 1)
                    nc.scalar.copy(XT[:, s.r % 2, :], bank(s.r % 2)[:, 0:P]).then_inc(bxt_ready, 1)
                if isinstance(s.n, int) and s.n < 1:
                    return
                b = s.back(1)
                act.wait_ge(hb_done, b.n + 1)
                nc.scalar.activation(HT[:, b.r % 2, :], HT[:, b.r % 2, :], ACT.Relu).then_inc(h_ready, 1)
            act.wait_ge(padr_in, 16)
            act.wait_ge(cnt_ready, 1)
            for e in range(E // 2, E):
                end = act.value_load(CNTI[0:1, e:e + 1], min_val=0, max_val=ROWS - P)
                act.dma_start(rows[bass.ds(end, P), :], PADR[:]).then_inc(pads_out, 16)
            act.wait_ge(lg_done, NS)
            steps(act, 0, NB + 1, 4, ffn, peel=4, tail=1)

        @block.vector
        def _(dve):
            dve.wait_ge(con_in, 16 * 12)
            dve.wait_ge(bo_mm, 1)
            nc.vector.tensor_tensor(BO[:], bank(0)[:, 0:D], BO[:], ALU.add).then_inc(bo_ready, 1)

            def moments(src, s, tiles, bufs, stat, half, gap, mv, done):
                n = s.n
                st, ms, mvs, _ = bufs
                need(dve, half, n)
                need(dve, mv, n)
                for t in range(tiles):
                    last = nc.vector.bn_stats(st[:, t, :], src(t))
                last.then_inc(stat, 1)
                dve.wait_ge(stat, n + 1)
                m0, m1, v0, v1 = (st[:, :, k] for k in (1, 4, 2, 5))
                nc.vector.tensor_tensor(ms[:, 0, :], m0, m1, ALU.add)
                nc.vector.tensor_tensor(ms[:, 1, :], v0, v1, ALU.add)
                nc.vector.tensor_tensor(ms[:, 2, :], m0, m1, ALU.subtract).then_inc(half, 1)
                dve.wait_ge(half, n + 1)
                need(dve, done, n + 1 - s.ring)
                nc.vector.tensor_scalar(mvs[:, s.r, 0, :], ms[:, 0, :], 0.5, None, ALU.mult)
                nc.vector.scalar_tensor_tensor(ms[:, 3, :], ms[:, 2, :], 0.25, ms[:, 2, :], ALU.mult, ALU.mult).then_inc(gap, 1)
                dve.wait_ge(gap, n + 1)
                nc.vector.scalar_tensor_tensor(mvs[:, s.r, 1, :], ms[:, 1, :], 1.0 / D, ms[:, 3, :], ALU.mult, ALU.add).then_inc(mv, 1)

            def normalise(src, dst, s, tiles, bufs, root, sd, rstd, done):
                n = s.n
                _, _, mvs, inv = bufs
                need(dve, done, n)
                dve.wait_ge(sd, n + 1)
                nc.vector.reciprocal(inv[:], root[:, s.r, :]).then_inc(rstd, 1)
                dve.wait_ge(rstd, n + 1)
                for t in range(tiles):
                    last = nc.vector.tensor_scalar(dst(t), src(t), mvs[:, s.r, 0, t:t + 1], inv[:, t:t + 1], ALU.subtract, ALU.mult)
                last.then_inc(done, 1)

            def stage1(s):
                whole = not isinstance(s.n, int)
                if whole or s.n < NG:
                    dve.wait_ge(x_in[s.r], 16 * (s.it + 1))
                    xg = X[:, bass.ds(s.n * GT, GT), :]
                    moments(lambda t: xg[:, t, :], s, GT, (STAT, MS, MV, RSTD), stat_done, half_done, gap_done, mv_done, xn_done)
                if whole or 1 <= s.n < NG + 1:
                    b = s.back(1)
                    need(dve, xt_done, b.n - 1)
                    xb = X[:, bass.ds(b.n * GT, GT), :]
                    normalise(lambda t: xb[:, t, :], lambda t: XN[:, b.r, t, :], b, GT, (STAT, MS, MV, RSTD), SD, sd_done, rstd_done, xn_done)
                if not whole and s.n < 2:
                    return
                b = s.back(2)
                dve.wait_ge(v_done, b.n + 1)
                nc.vector.tensor_copy(V[:, bass.ds(b.n * GW, GW)], bank(6 + b.r)).then_inc(v_kept, 1)
            steps(dve, 0, NG + 2, 2, stage1, peel=4, tail=2)

            def stage2(s):
                whole = not isinstance(s.n, int)
                if whole or s.n < NT:
                    sc = bank(2 * s.r, 2).rearrange("p (h k) -> p h k", h=H)
                    need(dve, sub_done, s.n - 1)
                    dve.wait_ge(s_done, s.n + 1)
                    nc.vector.tensor_reduce(MX[:, s.r, :], sc, axis=AX.X, op=ALU.max).then_inc(mx_done, 1)
                    dve.wait_ge(mx_done, s.n + 1)
                    need(dve, pt_done, s.n - 1)
                    nc.vector.tensor_tensor(SB[:, s.r].rearrange("p (h k) -> p h k", h=H), sc,
                                            MX[:, s.r, :].unsqueeze(2).to_broadcast([P, H, SEQ]), ALU.subtract).then_inc(sub_done, 1)
                if whole or s.n >= 3:
                    b = s.back(3)
                    dve.wait_ge(wo_done, b.n + 1)
                    xt = X[:, bass.ds(b.n, 1), :].rearrange("p a d -> p (a d)")
                    nc.vector.tensor_tensor(xt, bank(6 + b.r)[:, 256:384], xt, ALU.add).then_inc(x1_done, 1)
                if whole or 2 <= s.n < NT + 2:
                    b = s.back(2)
                    need(dve, ot_ready, b.n)
                    dve.wait_ge(od_done, b.n + 1)
                    nc.vector.reciprocal(RD[:], bank(6 + b.r)[:, 128:256]).then_inc(rd_done, 1)
                    dve.wait_ge(rd_done, b.n + 1)
                    need(dve, wo_done, b.n - 1)
                    nc.vector.tensor_tensor(OT[:, b.r, :], bank(6 + b.r)[:, 0:128], RD[:], ALU.mult).then_inc(ot_ready, 1)
            dve.wait_ge(xb_done, NG)
            steps(dve, 0, NT + 3, 2, stage2, peel=4, tail=3)

            for r in range(KR):
                dve.wait_ge(qs_in[r], 16 * (NT // KR))
            dve.wait_ge(vp_done, NT)
            dve.wait_ge(x1_done, NT)
            nc.vector.memset(HOT[:, ST, :], 0.0).then_inc(base_first, 1)
            nc.vector.tensor_copy(BASE[:], C[:, C_BASE:C_BASE + E]).then_inc(base_carry, 1)

            def stage3(s):
                whole = not isinstance(s.n, int)
                bufs = (STAT2, MS2, MV2, RSTD2)
                if whole or s.n < NS:
                    xg = X[:, bass.ds(s.n * ST, ST), :]
                    moments(lambda t: xg[:, t, :], s, ST, bufs, stat2, half2, gap2, mv2, xn2)
                b = s.back(1)
                if whole or s.n >= 1:
                    need(dve, dest_done, b.n)
                    need(dve, desti_done, b.n)
                    dve.wait_ge(lg_done, b.n + 1)
                    nc.vector.tensor_tensor(LG[:], bank(5)[:, 0:ST * E].rearrange("p (t e) -> p t e", e=E),
                                            BR[:].unsqueeze(1).to_broadcast([P, ST, E]), ALU.add).then_inc(lg_ready, 1)
                    dve.wait_ge(lg_ready, b.n + 1)
                    nc.vector.tensor_reduce(TOP[:], LG[:], axis=AX.X, op=ALU.max).then_inc(top_done, 1)
                    dve.wait_ge(top_done, b.n + 1)
                    nc.vector.tensor_tensor(PREF[:], LG[:], TOP[:].unsqueeze(2).to_broadcast([P, ST, E]), ALU.is_ge).then_inc(eq_done, 1)
                    dve.wait_ge(eq_done, b.n + 1)
                    nc.vector.tensor_tensor(LG[:], PREF[:], C[:, C_PREF:C_PREF + E].unsqueeze(1).to_broadcast([P, ST, E]), ALU.mult).then_inc(pref_done, 1)
                    dve.wait_ge(pref_done, b.n + 1)
                    nc.vector.tensor_reduce(TOP[:], LG[:], axis=AX.X, op=ALU.max).then_inc(best_done, 1)
                    dve.wait_ge(best_done, b.n + 1)
                    need(dve, rank_done, b.n)
                    nc.vector.tensor_tensor(HOT[:, 0:ST, :], LG[:], TOP[:].unsqueeze(2).to_broadcast([P, ST, E]), ALU.is_ge).then_inc(hot_done, 1)
                if whole or s.n < NS:
                    xg = X[:, bass.ds(s.n * ST, ST), :]
                    rg = RG[:, bass.ds(s.n * ST, ST), :]
                    normalise(lambda t: xg[:, t, :], lambda t: rg[:, t, 0:D], s, ST, bufs, SD2, sd2, rstd2, xn2)
                if whole or s.n >= 1:
                    dve.wait_ge(rank_done, b.n + 1)
                    dve.wait_ge(base_carry, b.n + 1)
                    dve.wait_ge(hot_done, b.n + 1)
                    nc.vector.tensor_tensor(POS[:], bank(4)[:, 0:(ST + 1) * E].rearrange("p (t e) -> p t e", e=E),
                                            BASE[:].unsqueeze(1).to_broadcast([P, ST + 1, E]), ALU.add).then_inc(pos_done, 1)
                    dve.wait_ge(pos_done, b.n + 1)
                    nc.vector.tensor_copy(BASE[:], POS[:, ST, :]).then_inc(base_carry, 1)
                    nc.vector.tensor_tensor(LG[:], POS[:, 0:ST, :], HOT[:, 0:ST, :], ALU.mult).then_inc(posm_done, 1)
                    dve.wait_ge(posm_done, b.n + 1)
                    nc.vector.tensor_reduce(DEST[:], LG[:], axis=AX.X, op=ALU.add).then_inc(dest_done, 1)
            steps(dve, 0, NS + 1, 1, stage3, peel=1, tail=1)

            dve.wait_ge(base_carry, NS + 1)
            nc.vector.tensor_copy(CNTI[:], BASE[0:1, :]).then_inc(cnt_ready, 1)
            made = [0]

            def link(ins):
                made[0] += 1
                ins.then_inc(tab_step, 1)
                dve.wait_ge(tab_step, made[0])

            def row(k):
                return TE[0:1, k, :]
            link(nc.vector.tensor_tensor(row(0), BASE[0:1, :], C[0:1, C_BASE:C_BASE + E], ALU.subtract))
            cm = CMP[0:1, 0:E * NT].rearrange("p (e m) -> p e m", e=E)
            link(nc.vector.tensor_tensor(cm, row(0).unsqueeze(2).to_broadcast([1, E, NT]),
                                         C[0:1, C_LIM:C_LIM + NT].unsqueeze(1).to_broadcast([1, E, NT]), ALU.is_gt))
            link(nc.vector.tensor_reduce(row(1), cm, axis=AX.X, op=ALU.add))
            src, dst = 1, 2
            for d in (1, 2, 4):
                link(nc.vector.tensor_copy(TE[0:1, dst, 0:d], TE[0:1, src, 0:d]))
                link(nc.vector.tensor_tensor(TE[0:1, dst, d:E], TE[0:1, src, d:E], TE[0:1, src, 0:E - d], ALU.add))
                src, dst = dst, dst + 1
            past = CMP[0:1, :].rearrange("p (i e) -> p i e", e=E)
            link(nc.vector.tensor_tensor(past, C[0:1, C_BLK:C_BLK + NB].unsqueeze(2).to_broadcast([1, NB, E]),
                                         row(src).unsqueeze(1).to_broadcast([1, NB, E]), ALU.is_ge))
            link(nc.vector.tensor_reduce(TB[0:1, 0, :], past, axis=AX.X, op=ALU.add))
            link(nc.vector.tensor_tensor(past, past, row(1).unsqueeze(1).to_broadcast([1, NB, E]), ALU.mult))
            link(nc.vector.tensor_reduce(TB[0:1, 1, :], past, axis=AX.X, op=ALU.add))
            link(nc.vector.tensor_tensor(TB[0:1, 2, :], C[0:1, C_BLK:C_BLK + NB], TB[0:1, 1, :], ALU.subtract))
            link(nc.vector.tensor_scalar(TB[0:1, 1, :], TB[0:1, 0, :], float(CAP), None, ALU.mult))
            link(nc.vector.scalar_tensor_tensor(TB[0:1, 3, :], TB[0:1, 2, :], float(P), TB[0:1, 1, :], ALU.mult, ALU.add))
            link(nc.vector.tensor_copy(TABI[:, 0, :], TB[0:1, 3, :]))
            link(nc.vector.tensor_scalar(TB[0:1, 2, :], TB[0:1, 0, :], float(E - 1), None, ALU.min))
            nc.vector.tensor_copy(TABI[:, 1, :], TB[0:1, 2, :]).then_inc(tab_ready, 1)

            dve.wait_ge(w2_in, 48)
            dve.wait_ge(tab_ready, 1)
            def ffn(s):
                whole = not isinstance(s.n, int)
                if whole or s.n < NB:
                    ex = dve.value_load(TABI[0:1, 1, bass.ds(s.n, 1)], min_val=0, max_val=E - 1)
                    dve.wait_ge(h_done, s.n + 1)
                    need(dve, y_done, s.n - 1)
                    nc.vector.tensor_tensor(HT[:, s.r % 2, :].rearrange("p (c t) -> p c t", c=FC),
                                            bank(2 + s.r % 2).rearrange("p (c t) -> p c t", c=FC),
                                            B1[:, bass.ds(ex, 1), :].rearrange("p a c -> p (a c)").unsqueeze(2).to_broadcast([P, FC, P]),
                                            ALU.add).then_inc(hb_done, 1)
                if whole or s.n >= 1:
                    b = s.back(1)
                    exb = dve.value_load(TABI[0:1, 1, bass.ds(b.n, 1)], min_val=0, max_val=E - 1)
                    need(dve, y_out[b.r], 16 * b.it)
                    dve.wait_ge(y_done, b.n + 1)
                    nc.vector.tensor_tensor(YO[:, b.r, :], bank(4 + b.r % 2)[:, 0:D],
                                            B2[:, bass.ds(exb, 1), :].rearrange("p a c -> p (a c)"), ALU.add).then_inc(yx_done, 1)
                    dve.wait_ge(yx_done, b.n + 1)
                    nc.vector.tensor_tensor(YO[:, b.r, :], YO[:, b.r, :], RT[:, b.r, D:2 * D], ALU.add).then_inc(yo_ready, 1)
            steps(dve, 0, NB + 1, RR, ffn, peel=RR, tail=1)

        @block.tensor
        def _(pe):
            pe.wait_ge(con_in, 16 * 12)
            nc.tensor.matmul(bank(0)[:, 0:D], BV[:], WO[:], start=True, stop=True).then_inc(bo_mm, 1)
            pe.wait_ge(bo_ready, 1)

            def stage1(s):
                whole = not isinstance(s.n, int)
                pe.wait_ge(xn_done, s.n + 1)
                need(pe, xnt_ready, s.n - 1)
                for t in range(GT):
                    last = nc.tensor.transpose(bank(s.r)[:, t * P:(t + 1) * P], XN[:, s.r, t, :], ident)
                last.then_inc(xt_done, 1)
                pe.wait_ge(ct_in[s.r], 16 * (s.it + 1))
                need(pe, k_kept, s.n - 1)
                nc.tensor.matmul(bank(4 + s.r), WK[:], CT[:, s.r, :], start=True, stop=True).then_inc(k_done, 1)
                need(pe, v_kept, s.n - 1)
                for b in range(2 * GT):
                    for r in range(2):
                        h = slice(SEQ * r, SEQ * r + SEQ)
                        last = nc.tensor.matmul(bank(6 + s.r)[h, b * SEQ:(b + 1) * SEQ], CT[:, s.r, b * SEQ:(b + 1) * SEQ],
                                                WV[:, h], start=True, stop=True)
                last.then_inc(v_done, 1)
                pe.wait_ge(xnt_ready, s.n + 1)
                need(pe, q_kept, s.n - 1)
                nc.tensor.matmul(bank(2 + s.r), WQ[:], XNT[:, s.r, :], start=True, stop=True).then_inc(q_done, 1)
            steps(pe, 0, NG, 2, stage1, peel=2)

            pe.wait_ge(q_kept, NG)
            pe.wait_ge(v_kept, NG)
            ob = C[:, C_OB:C_OB + 64].rearrange("p (s m) -> p s m", s=2)

            def stage2(s):
                whole = not isinstance(s.n, int)
                if whole or s.n < NT:
                    pe.wait_ge(qs_in[s.r], 16 * (s.it + 1))
                    pe.wait_ge(km_in[s.r], 64 * (s.it + 1))
                    need(pe, sub_done, s.n - 1)
                    for half in range(2):
                        for b in range(2):
                            q = QS[:, s.r, SEQ * b:SEQ * b + SEQ]
                            k = KM[:, s.r, b, 8 * half:8 * half + 8, :]
                            last = nc.tensor.matmul(bank(2 * (s.r % 2) + half)[SEQ * b:SEQ * b + SEQ, :], q, k, start=True, stop=True)
                    last.then_inc(s_done, 1)
                if whole or s.n >= 3:
                    b3 = s.back(3)
                    pe.wait_ge(ot_ready, b3.n + 1)
                    nc.tensor.matmul(bank(6 + b3.r % 2)[:, 256:384], OT[:, b3.r % 2, :], WO[:], start=True, stop=True).then_inc(wo_done, 1)
                if whole or 1 <= s.n < NT + 1:
                    b1 = s.back(1)
                    pe.wait_ge(exp_done, b1.n + 1)
                    need(pe, pt_ready, b1.n)
                    for hp in range(HP):
                        last = nc.tensor.transpose(bank(4, 2)[:, hp * P:(hp + 1) * P], SB[:, b1.r % 2, hp * P:(hp + 1) * P], ident)
                    last.then_inc(pt_done, 1)
                if whole or 2 <= s.n < NT + 2:
                    b2 = s.back(2)
                    pe.wait_ge(pt_ready, b2.n + 1)
                    pe.wait_ge(vp_done, b2.n + 1)
                    need(pe, x1_done, b2.n - 1)
                    for b in range(2):
                        for z in range(2):
                            for c in range(4):
                                nc.tensor.matmul(bank(6 + b2.r % 2)[32 * c:32 * c + 32, SEQ * b:SEQ * b + SEQ],
                                                 VP[:, b2.r % 2, b, 2 * c + z, :], PT[:, b2.r % 2, 2 * c + z, SEQ * b:SEQ * b + SEQ],
                                                 start=z == 0, stop=z == 1)
                    for z in range(2):
                        for c in range(4):
                            last = nc.tensor.matmul(bank(6 + b2.r % 2)[32 * c:32 * c + 32, P:2 * P], ob[:, z, :],
                                                    PT[:, b2.r % 2, 2 * c + z, :], start=z == 0, stop=z == 1)
                    last.then_inc(od_done, 1)
            steps(pe, 0, NT + 3, KR, stage2, peel=4, tail=3)

            pe.wait_ge(sub_done, NT)
            pe.wait_ge(x1_done, NT)
            pe.wait_ge(pt_ready, NT)
            pe.wait_ge(base_first, 1)
            def stage3(s):
                whole = not isinstance(s.n, int)
                if whole or s.n >= 1:
                    b = s.back(1)
                    pe.wait_ge(hot_done, b.n + 1)
                    need(pe, pos_done, b.n)
                    sums = bank(4)[:, 0:(ST + 1) * E]
                    nc.tensor.matmul(sums, tri, HOT[:].rearrange("p t e -> p (t e)"), start=True, stop=False)
                    for t in range(ST):
                        last = nc.tensor.matmul(sums[:, (t + 1) * E:].rearrange("p (t e) -> p t e", e=E), ones,
                                                HOT[:, t:t + 1, :].to_broadcast([P, ST - t, E]), start=False, stop=t == ST - 1)
                    last.then_inc(rank_done, 1)
                if whole or s.n < NS:
                    pe.wait_ge(xn2, s.n + 1)
                    for j in range(4):
                        need(pe, x1t_ready, s.n * 4 - 3 + j)
                        for t in range(GT):
                            last = nc.tensor.transpose(bank(j)[:, t * P:(t + 1) * P], RG[:, s.n * ST + j * GT + t, 0:D], ident)
                        last.then_inc(xt2_done, 1)
                    need(pe, lg_ready, s.n)
                    for t in range(ST):
                        if t % GT == 0:
                            pe.wait_ge(x1t_ready, s.n * 4 + t // GT + 1)
                        last = nc.tensor.matmul(bank(5)[:, t * E:(t + 1) * E], X1T[:, t * P:(t + 1) * P], WR[:], start=True, stop=True)
                    last.then_inc(lg_done, 1)
            steps(pe, 0, NS + 1, NS, stage3)

            pe.wait_ge(w2_in, 48)
            pe.wait_ge(tab_ready, 1)
            def transpose_rows(s):
                whole = not isinstance(s.n, int)
                pe.wait_ge(rt_in[s.r], 16 * (s.it + 1))
                need(pe, bxt_ready, s.n - 1)
                nc.tensor.transpose(bank(s.r % 2)[:, 0:P], RT[:, s.r, 0:D], ident).then_inc(bx_done, 1)

            def ffn(s):
                whole = not isinstance(s.n, int)
                if whole or s.n < NB:
                    transpose_rows(s)
                if whole or 1 <= s.n < NB + 1:
                    b = s.back(1)
                    pe.wait_ge(bxt_ready, b.n + 1)
                    pe.wait_ge(w1_in[b.r % 4], 16 * (2 * b.it + b.r // 4 + 1))
                    need(pe, hb_done, b.n - 1)
                    for c in range(FC):
                        last = nc.tensor.matmul(bank(2 + b.r % 2)[:, c * P:(c + 1) * P], W1S[:, b.r % 4, c * P:(c + 1) * P],
                                                XT[:, b.r % 2, :], start=True, stop=True)
                    last.then_inc(h_done, 1)
                if whole or s.n >= 2:
                    b = s.back(2)
                    ex = pe.value_load(TABI[0:1, 1, bass.ds(b.n, 1)], min_val=0, max_val=E - 1)
                    pe.wait_ge(h_ready, b.n + 1)
                    need(pe, yx_done, b.n - 1)
                    for c in range(FC):
                        w = W2[:, bass.ds(ex, 1), c, :].rearrange("p a d -> p (a d)")
                        last = nc.tensor.matmul(bank(4 + b.r % 2)[:, 0:D], HT[:, b.r % 2, c * P:(c + 1) * P], w,
                                                start=c == 0, stop=c == FC - 1)
                    last.then_inc(y_done, 1)
            steps(pe, 0, NB + 2, RR, ffn, peel=RR, tail=2)


def kernel(x, ctx_1024, L0_xattn_Wq, L0_xattn_bq, L0_xattn_Wk, L0_xattn_bk, L0_xattn_Wv, L0_xattn_bv,
           L0_xattn_Wo, L0_xattn_bo, L0_ffn_Wr, L0_ffn_br, L0_ffn_W1, L0_ffn_b1, L0_ffn_W2, L0_ffn_b2):
    import concourse.bacc as bacc
    from concourse.bass_utils import run_bass_kernel_spmd

    def lay(a):
        return np.ascontiguousarray(a)

    con, pad, ids = constants()
    n = np.asarray
    arrays = {
        "x": lay(n(x).reshape(TOK, D)),
        "ctxT": lay(n(ctx_1024).reshape(TOK, D).T),
        "wq": lay(n(L0_xattn_Wq).T), "wk": lay(n(L0_xattn_Wk).T),
        "wv": lay(n(L0_xattn_Wv).reshape(HP, 2, DK, D).transpose(3, 1, 0, 2).reshape(D, D)), "wo": lay(n(L0_xattn_Wo).T),
        "bq": lay(n(L0_xattn_bq).reshape(D, 1)), "bk": lay(n(L0_xattn_bk).reshape(D, 1)),
        "bv": lay(np.broadcast_to(n(L0_xattn_bv)[:, None], (D, P))),
        "bo": lay(np.broadcast_to(n(L0_xattn_bo)[None], (P, D))),
        "wr": lay(n(L0_ffn_Wr).T), "br": lay(np.broadcast_to(n(L0_ffn_br)[None], (P, E))),
        "w1": lay(n(L0_ffn_W1).transpose(2, 0, 1).reshape(D, E * F)),
        "b1": lay(n(L0_ffn_b1).reshape(E, FC, P).transpose(2, 0, 1)),
        "w2": lay(n(L0_ffn_W2).reshape(E, D, FC, P).transpose(3, 0, 2, 1)),
        "b2": lay(np.broadcast_to(n(L0_ffn_b2)[None], (P, E, D))),
        "con": con, "pad": pad, "ids": ids,
    }
    nc = bacc.Bacc("TRN2", target_bir_lowering=False, num_devices=1)
    args = [nc.dram_tensor("in_" + k, a.shape, mybir.dt.from_np(a.dtype), kind="ExternalInput").ap()
            for k, a in arrays.items()]
    out = nc.dram_tensor("out", (TOK, D), mybir.dt.float32, kind="ExternalOutput").ap()
    build(nc, *args, out)
    r = run_bass_kernel_spmd(nc, [{"in_" + k: a for k, a in arrays.items()}], core_ids=[0])
    return r.results[0]["out"].reshape(BATCH, SEQ, D)
```

```python
import concourse.bass as bass
from concourse import mybir
from contextlib import ExitStack
import numpy as np

P = 128
D = 128
SEQ = 64
BATCH = 128
TOK = BATCH * SEQ
NT = TOK // P
GT = 4
NG = NT // GT
GW = GT * P
H = 16
DK = D // H
HP = H // 2
E = 8
F = 512
FC = F // P
CAP = TOK + P
NB = TOK // P + E - 1
PADS = NB - TOK // P
ROWS = E * CAP + PADS * P
KR = 4
ST = 8
NS = NT // ST
RR = 8
ID, MU, RS = D, D + 1, D + 2
RW = D + 4
WEW = F + FC + D
EPS = 1e-5
SCALE = float(1.0 / np.sqrt(np.float32(DK)))

C_ID, C_TRI, C_ONE, C_OB, C_JM, C_PREF, C_BASE, C_LIM, C_BLK, C_EPS, C_1H, C_END = np.cumsum(
    [0, P, P, P, 2 * 32, 4 * SEQ, E, E, NT, NB, 1, ST]).tolist()
(W_Q, W_K, W_V, W_BQ, W_BK, W_O, W_BV, W_BO, W_R, W_BR, W_END) = np.cumsum(
    [0, D, D, D, 1, 1, D, P, D, E, E]).tolist()


def constants():
    c = np.zeros((P, C_END), np.float32)
    p = np.arange(P)
    c[:, C_ID:C_ID + P] = np.eye(P)
    c[:, C_TRI:C_TRI + P] = p[:, None] < p[None, :]
    c[:, C_ONE:C_ONE + P] = 1
    for s in range(2):
        for r in range(2):
            a = C_OB + 32 * s + 16 * s + DK * r
            c[SEQ * r:SEQ * r + SEQ, a:a + DK] = 1
    for j in range(4):
        c[(p // DK) % 4 == j, C_JM + SEQ * j:C_JM + SEQ * (j + 1)] = 1
    c[:, C_PREF:C_PREF + E] = E - np.arange(E)
    c[:, C_BASE:C_BASE + E] = CAP * np.arange(E)
    c[:, C_LIM:C_LIM + NT] = P * np.arange(NT)
    c[:, C_BLK:C_BLK + NB] = np.arange(NB)
    c[:, C_EPS] = EPS
    c[:, C_1H:C_1H + ST] = 1.5
    pad = np.zeros((P, RW), np.float32)
    pad[:, ID] = np.full(P, TOK, np.int32).view(np.float32)
    ids = np.ascontiguousarray(np.arange(TOK, dtype=np.int32).reshape(NT, P).T)
    return c, pad, ids


M_BN = 4
M_MOM = 11
M_INV = (15, 16)
M_SEED = 12
M_CEN = 14
M_TR = 16
M_LG = 17
M_TOP = 22
M_HOT = 23
M_RANK = 23
M_POS = 24
INV_STEPS = 12
M_XR = 24
M_OUT = M_XR + 3
RK = 2 * P + ST * E
STEPS = NT - ST + M_OUT + ST // 2


class Step:

    def __init__(self, it, r, ring):
        self.it, self.r, self.ring = it, r, ring
        self.n = it * ring + r

    def back(self, k):
        q, r = divmod(self.r - k, self.ring)
        return Step(self.it + q if q else self.it, r, self.ring)

    def turn(self, k):
        return self.it * (self.ring // k) + self.r // k + 1

    def batch(self, m):
        if self.r != m % ST:
            return None
        j = self.it - m // ST if m >= ST else self.it
        return None if isinstance(j, int) and not 0 <= j < NS else j

    def last_batch(self, m):
        return isinstance(self.it, int) and self.batch(m) == NS - 1


def need(eng, sem, value):
    if not isinstance(value, int) or value > 0:
        eng.wait_ge(sem, value)


def steps(eng, first, last, ring, body, peel=0, tail=0):
    lo = -(-max(first, peel) // ring)
    hi = (last - tail) // ring
    for n in range(first, lo * ring):
        body(Step(n // ring, n % ring, ring))
    if hi - lo > 1:
        with eng.Fori(lo, hi) as it:
            for r in range(ring):
                body(Step(it, r, ring))
    else:
        hi = lo
    for n in range(hi * ring, last):
        body(Step(n // ring, n % ring, ring))


def build(nc, x, ctxT, wts, we, w2, con, pad, ids, out):
    f32, i32 = mybir.dt.float32, mybir.dt.int32
    ALU, ACT, AX = mybir.AluOpType, mybir.ActivationFunctionType, mybir.AxisListType
    x_v = x.rearrange("(t p) d -> p t d", p=P)
    rows = nc.dram_tensor("rows", (ROWS, RW), f32).ap()

    ctx = ExitStack()
    with ctx:
        def sb(name, *shape, dt=f32):
            return ctx.enter_context(nc.sbuf_tensor(name, list(shape), dt))

        def sem(name):
            return ctx.enter_context(nc.semaphore(name))

        def sems(name, n):
            return [sem(f"{name}{i}") for i in range(n)]

        X = sb("X", P, NT, RW)
        BIG = sb("BIG", P, 3 * TOK)
        QT = BIG[:, 0:TOK]
        KT = BIG[:, TOK:2 * TOK]
        V = BIG[:, 2 * TOK:3 * TOK]
        C = sb("C", P, C_END)
        ident = C[:, C_ID:C_ID + P]
        W = sb("W", P, W_END)
        WQ, WK, WV, WO, BV = (W[:, a:a + D] for a in (W_Q, W_K, W_V, W_O, W_BV))
        BO = W[:, W_BO:W_BO + D]
        BQK = W[:, W_BQ:W_BQ + 2]
        WR, BR = W[:, W_R:W_R + E], W[:, W_BR:W_BR + E]
        XC = sb("XC", P, ST, D)
        X1T = sb("X1T", P, 4, 2, P)
        STAT2, MS2 = sb("STAT2", P, ST, 6), sb("MS2", P, 4, ST)
        MINUS, VAR2 = sb("MINUS", P, ST), sb("VAR2", P, ST)
        HALF, Y, YY = sb("HALF", P, ST), sb("Y", P, ST), sb("YY", P, ST)
        LG, PREF = sb("LG", P, ST, E), sb("PREF", P, ST, E)
        TOP = sb("TOP", P, ST)
        HOT = sb("HOT", P, ST + 1, E, dt=mybir.dt.bfloat16)
        COUNT = sb("COUNT", P, 2, P, dt=mybir.dt.bfloat16)
        XR = sb("XR", P, 4, RW)
        BASE = sb("BASE", P, E)
        POS = sb("POS", P, ST + 1, E)
        DEST = sb("DEST", P, ST)
        STAT, MS = sb("STAT", P, GT, 6), sb("MS", P, 4, GT)
        MV = sb("MV", P, 2, 2, GT)
        SD, RSTD = sb("SD", P, 2, GT), sb("RSTD", P, GT)
        QS = sb("QS", P, KR, P)
        KJ = sb("KJ", P, 2, 2, 4, SEQ)
        KM = sb("KM", P, KR, 2, H, SEQ)
        SB = sb("SB", P, 2, H * SEQ)
        MX = sb("MX", P, 2, H)
        PT = sb("PT", P, 2, HP, P)
        XN = SB[:].rearrange("p r (t d) -> p (r t) d", d=D)[:, 0:2 * GT, :].rearrange("p (r t) d -> p r t d", r=2)
        XNT = SB[:, 1, :].rearrange("p (r w) -> p r w", r=2)
        CT = PT[:].rearrange("p r (k a) d -> p (r k) (a d)", k=2)
        VP = sb("VP", P, 2, 2, HP, 32)
        RD = sb("RD", P, P)
        OT = sb("OT", P, 2, P)

        def big(at, *shape):
            n = int(np.prod(shape))
            v = BIG[:, at:at + n]
            if len(shape) == 2:
                v = v.rearrange("p (a b) -> p a b", a=shape[0])
            if len(shape) == 3:
                v = v.rearrange("p (a b c) -> p a b c", a=shape[0], b=shape[1])
            return v, at + n

        at = 0
        PADR, at = big(at, RW)
        CMP, at = big(at, NB * E)
        TE, at = big(at, 6, E)
        TB, at = big(at, 4, NB)
        TABI, at = big(at, 2, NB)
        TABI = TABI[0:1].bitcast(i32)
        WE, at = big(at, E, WEW)
        RT, at = big(at, RR, RW)
        RN, at = big(at, 4, P)
        XT, at = big(at, 2, P)
        km = KM[:].rearrange("p r b h k -> p (r b h k)")
        W2 = km[:, 0:E * F].rearrange("p (e c d) -> p e c d", e=E, c=FC)
        WS = km[:, E * F:E * F + 4 * WEW].rearrange("p (r f) -> p r f", r=4)
        HT = SB[:, 0, :].rearrange("p (r f) -> p r f", r=2)
        YO = SB[:, 1, :].rearrange("p (r d) -> p r d", r=RR)
        assert at <= 3 * TOK
        IDS = sb("IDS", P, NT, dt=i32)
        DESTI = sb("DESTI", P, ST, dt=i32)
        CNTI = sb("CNTI", 1, E, dt=i32)

        PS = ctx.enter_context(nc.psum_tensor("PS", [P, 8 * 512], f32))

        def bank(k, n=1):
            return PS[:, 512 * k:512 * (k + n)]

        con_in, w_in, ids_in, w2_in = sem("con_in"), sem("w_in"), sem("ids_in"), sem("w2_in")
        x_in, ct_in = sems("x_in", 4), sems("ct_in", 4)
        stat_done, mv_done, sd_done, rstd_done, xn_done = (sem(n) for n in ("stat_done", "mv_done", "sd_done", "rstd_done", "xn_done"))
        xt_done, xnt_ready = sem("xt_done"), sem("xnt_ready")
        q_done, k_done, v_done = sem("q_done"), sem("k_done"), sem("v_done")
        q_kept, k_kept, v_kept = sem("q_kept"), sem("k_kept"), sem("v_kept")
        bo_mm, bo_ready, xb_done = sem("bo_mm"), sem("bo_ready"), sem("xb_done")
        zeroed = sem("zeroed")
        qs_in, km_in = sems("qs_in", KR), sems("km_in", KR)
        kj_done, vp_done = sem("kj_done"), sem("vp_done")
        s_done, mx_done, sub_done, exp_done = (sem(n) for n in ("s_done", "mx_done", "sub_done", "exp_done"))
        pt_done, pt_ready, od_done, rd_done, ot_ready = (sem(n) for n in ("pt_done", "pt_ready", "od_done", "rd_done", "ot_ready"))
        wo_done, x1_done = sem("wo_done"), sem("x1_done")
        half_done, gap_done, half2, gap2 = (sem(n) for n in ("half_done", "gap_done", "half2", "gap2"))
        stat2, mv2, inv_step, xc_done, scaled = (sem(n) for n in ("stat2", "mv2", "inv_step", "xc_done", "scaled"))
        seed_step = sem("seed_step")
        id_done, xt2_done, x1t_ready = (sem(n) for n in ("id_done", "xt2_done", "x1t_ready"))
        lgp_done, lg_ready, top_done, eq_done, pref_done, best_done, hot_done = (
            sem(n) for n in ("lgp_done", "lg_ready", "top_done", "eq_done", "pref_done", "best_done", "hot_done"))
        rank_done, zero_row, pos_done, posm_done, dest_done, desti_done = (
            sem(n) for n in ("rank_done", "zero_row", "pos_done", "posm_done", "dest_done", "desti_done"))
        base_carry = sem("base_carry")
        routed, sent, xr_ready = sems("routed", 4), sem("sent"), sem("xr_ready")
        padr_in, pads_out = sem("padr_in"), sem("pads_out")
        cnt_ready, tab_step, tab_ready = sem("cnt_ready"), sem("tab_step"), sem("tab_ready")
        rt_in, ws_ready, y_out = sems("rt_in", RR), sem("ws_ready"), sems("y_out", RR)
        we_in, rn_done = sem("we_in"), sem("rn_done")
        bx_done, bxt_ready, h_done, hb_done, h_ready = (sem(n) for n in ("bx_done", "bxt_ready", "h_done", "hb_done", "h_ready"))
        y_done, yx_done, yo_ready = sem("y_done"), sem("yx_done"), sem("yo_ready")

        def tr_bank(j, i):
            return i if isinstance(j, int) and j == NS - 1 else 7

        block = ctx.enter_context(nc.Block())

        @block.sync
        def _(sp):
            def load_group(s):
                def go(before):
                    if before:
                        sp.wait_ge(stat_done, s.n - 3)
                    sp.dma_start(X[:, bass.ds(s.n * GT, GT), 0:D], x_v[:, bass.ds(s.n * GT, GT), :]).then_inc(x_in[s.r], 16)
                    if isinstance(s.n, int) and s.n == 0:
                        sp.dma_start(C[:], con).then_inc(con_in, 16)
                        sp.dma_start(W[:], wts).then_inc(w_in, 16)
                        sp.dma_start(IDS[:], ids).then_inc(ids_in, 16)
                    if before:
                        sp.wait_ge(v_done, s.n - 3)
                        sp.wait_ge(k_done, s.n - 3)
                    sp.dma_start(CT[:, s.r, :], ctxT[:, bass.ds(s.n * GW, GW)]).then_inc(ct_in[s.r], 16)
                go(not isinstance(s.n, int) or s.n >= 4)
            steps(sp, 0, NG, 4, load_group, peel=4)

            sp.wait_ge(zeroed, 2)
            sp.wait_ge(q_kept, 1)
            def spread(s):
                need(sp, s_done, s.n - KR + 1)
                sp.dma_start(QS[:, s.r, :], QT[:, bass.ds(s.n * P, P)]).then_inc(qs_in[s.r], 16)
                sp.wait_ge(kj_done, s.n + 1)
                for g in range(4):
                    r = slice(32 * g, 32 * g + 32)
                    sp.dma_start(KM[r, s.r, :, 4 * g:4 * g + 4, :], KJ[r, s.r % 2]).then_inc(km_in[s.r], 16)
            for n in range(KR):
                spread(Step(0, n, KR))
            sp.wait_ge(q_kept, NG)
            steps(sp, KR, NT, KR, spread, peel=4)

            sp.wait_ge(s_done, NT)
            sp.dma_start(W2, w2).then_inc(w2_in, 16)
            sp.wait_ge(vp_done, NT)
            for r in range(KR):
                sp.wait_ge(qs_in[r], 16 * (NT // KR))
            sp.dma_start(PADR[:], pad).then_inc(padr_in, 16)
            sp.dma_start(WE[:], we).then_inc(we_in, 16)
            sp.wait_ge(padr_in, 16)
            for k in range(PADS):
                sp.dma_start(rows[E * CAP + k * P:E * CAP + (k + 1) * P, :], PADR[:]).then_inc(pads_out, 16)
            sp.wait_ge(cnt_ready, 1)
            for e in range(E):
                end = sp.value_load(CNTI[0:1, e:e + 1], min_val=0, max_val=ROWS - P)
                sp.dma_start(rows[bass.ds(end, P), :], PADR[:]).then_inc(pads_out, 16)

            sp.wait_ge(tab_ready, 1)
            sp.wait_ge(pads_out, 16 * (PADS + E))
            def load_block(s):
                whole = not isinstance(s.n, int)
                if whole or s.n < NB:
                    row = sp.value_load(TABI[0:1, 0, bass.ds(s.n, 1)], min_val=0, max_val=ROWS - P)
                    if isinstance(s.n, int) and s.n == 0:
                        for q in range(4):
                            sp.wait_ge(routed[q], 16 * NT // 4)
                    need(sp, y_out[s.r], 16 * s.it)
                    sp.dma_start(RT[:, s.r, :], rows[bass.ds(row, P), :]).then_inc(rt_in[s.r], 16)
            steps(sp, 0, NB, RR, load_block, peel=RR)

        @block.gpsimd
        def _(pool):
            nc.gpsimd.memset(KM[:], 0.0).then_inc(zeroed, 1)
            nc.gpsimd.memset(VP[:], 0.0).then_inc(zeroed, 1)

            pool.wait_ge(ids_in, 16)
            nc.gpsimd.tensor_copy(X[:, :, ID:ID + 1].bitcast(i32), IDS[:].unsqueeze(2)).then_inc(id_done, 1)
            nc.gpsimd.memset(X[:, :, RS + 1:RW], 0.0).then_inc(id_done, 1)

            pool.wait_ge(bo_ready, 1)
            def add_bias(s):
                pool.wait_ge(xn_done, s.n + 1)
                g = X[:, bass.ds(s.n * GT, GT), 0:D]
                nc.gpsimd.tensor_tensor(g, g, BO.unsqueeze(1).to_broadcast([P, GT, D]), ALU.add).then_inc(xb_done, 1)

            jmask = C[:, C_JM:C_JM + 4 * SEQ].rearrange("p (j k) -> p j k", j=4)
            def copies(s):
                whole = not isinstance(s.n, int)
                b2 = s.back(2)
                if whole or b2.n >= 0:
                    pool.wait_ge(km_in[b2.r % KR], 64 * b2.turn(KR))
                for b in range(2):
                    k = KT[:, bass.ds(s.n * P + SEQ * b, SEQ)].unsqueeze(1).to_broadcast([P, 4, SEQ])
                    last = nc.gpsimd.tensor_tensor(KJ[:, s.r % 2, b], k, jmask, ALU.mult)
                last.then_inc(kj_done, 1)
            steps(pool, 0, NG - 4, 2, add_bias)
            pool.wait_ge(k_kept, 1)
            for n in range(KR):
                copies(Step(0, n, ST))
                add_bias(Step(0, NG - 4 + n, NG))
            pool.wait_ge(k_kept, NG)
            pool.wait_ge(v_kept, NG)
            pool.wait_ge(zeroed, 2)
            pool.wait_ge(id_done, 2)
            last_row, last_token = pool.to_reg(ROWS - 1), pool.to_reg(TOK - 1)
            def newton(j, first, last):
                for k in range(first, last):
                    turn, part = divmod(k, 4)
                    if part == 0:
                        op = nc.gpsimd.tensor_tensor(YY[:], Y[:], Y[:], ALU.mult)
                    elif part == 1:
                        op = nc.gpsimd.tensor_tensor(YY[:], YY[:], HALF[:], ALU.mult)
                    elif part == 2:
                        op = nc.gpsimd.tensor_tensor(YY[:], C[:, C_1H:C_1H + ST], YY[:], ALU.subtract)
                    else:
                        end = Y[:] if turn < INV_STEPS // 4 - 1 else X[:, bass.ds(j * ST, ST), RS]
                        op = nc.gpsimd.tensor_tensor(end, YY[:], Y[:], ALU.mult)
                    op.then_inc(inv_step, 1)
                    pool.wait_ge(inv_step, INV_STEPS * j + k + 1)

            def masks(s):
                whole = not isinstance(s.n, int)
                if whole or KR <= s.n < NT:
                    copies(s)
                if whole or 3 <= s.n < NT + 3:
                    t = s.back(3)
                    need(pool, od_done, t.n - 1)
                    for z in range(2):
                        dst = VP[:, t.r % 2].rearrange("p b (c z) m -> p (b c) z m", z=2)[:, :, z, 16 * z:16 * z + 16].rearrange("p g (r w) -> p g r w", w=DK)
                        v = V[:, bass.ds(t.n * P, P)].rearrange("p (g z w) -> p g z w", z=2, w=DK)[:, :, z, :].unsqueeze(2).to_broadcast([P, 8, 2, DK])
                        own = C[:, C_OB:C_OB + 16].rearrange("p (r w) -> p r w", w=DK).unsqueeze(1).to_broadcast([P, 8, 2, DK])
                        last = nc.gpsimd.tensor_tensor(dst, v, own, ALU.mult)
                    last.then_inc(vp_done, 1)
                j = s.batch(M_OUT)
                if j is not None:
                    pool.wait_ge(dest_done, j + 1)
                    for q in range(4):
                        need(pool, routed[q], 16 * (ST // 4) * j)
                    pool.sem_inc(sent, 1)
                    nc.gpsimd.tensor_copy(DESTI[:], DEST[:]).then_inc(desti_done, 1)
                    pool.wait_ge(desti_done, j + 1)
                    pool.sem_inc(sent, 1)
                j = s.batch(M_INV[0])
                if j is not None:
                    pool.wait_ge(seed_step, 4 * j + 4)
                    newton(j, 0, 6)
                j = s.batch(M_INV[1])
                if j is not None:
                    newton(j, 6, INV_STEPS)
                for t in range(ST):
                    j = s.batch(M_OUT + t // 2)
                    if j is not None:
                        pool.wait_ge(xr_ready, j * ST + t + 1)
                        pool.sem_inc(sent, 1)
                        nc.gpsimd.indirect_dma_start(
                            out=rows, out_offset=bass.IndirectOffsetOnAxis(ap=DESTI[:, t:t + 1], axis=0),
                            in_=XR[:, t % 4, :], in_offset=None,
                            bounds_check=last_row, oob_is_err=False).then_inc(routed[t % 4], 16)
            steps(pool, 0, STEPS, ST, masks, peel=32, tail=STEPS - NT)

            def home(s):
                pool.wait_ge(yo_ready, s.n + 1)
                pool.sem_inc(sent, 1)
                nc.gpsimd.indirect_dma_start(
                    out=out, out_offset=bass.IndirectOffsetOnAxis(ap=RT[:, s.r, ID:ID + 1].bitcast(i32), axis=0),
                    in_=YO[:, s.r, :], in_offset=None, bounds_check=last_token, oob_is_err=False).then_inc(y_out[s.r], 16)
            steps(pool, 0, NB, RR, home)
            for r in range(RR):
                pool.wait_ge(y_out[r], 16 * len(range(r, NB, RR)))

        @block.scalar
        def _(act):
            act.wait_ge(con_in, 16)

            def root(n, dst, src, slots, mv, sd, rstd):
                need(act, rstd, n + 1 - slots)
                act.wait_ge(mv, n + 1)
                nc.scalar.activation(dst, src, ACT.Sqrt, bias=C[:, C_EPS:C_EPS + 1]).then_inc(sd, 1)

            def keep(t):
                whole = not isinstance(t.n, int)
                if whole or t.n < NG:
                    root(t.n, SD[:, t.r, :], MV[:, t.r, 1, :], 2, mv_done, sd_done, rstd_done)
                if not whole and t.n < 1:
                    return
                s = t.back(1)
                act.wait_ge(xt_done, s.n + 1)
                need(act, q_done, s.n - 1)
                nc.scalar.copy(XNT[:, s.r, :], bank(s.r)).then_inc(xnt_ready, 1)
                if isinstance(s.n, int) and s.n == 0:
                    act.wait_ge(w_in, 16)
                act.wait_ge(k_done, s.n + 1)
                nc.scalar.activation(KT[:, bass.ds(s.n * GW, GW)], bank(4 + s.r), ACT.Identity, bias=BQK[:, 1:2]).then_inc(k_kept, 1)
                act.wait_ge(v_done, s.n + 1)
                nc.scalar.copy(V[:, bass.ds(s.n * GW, GW)], bank(6 + s.r)).then_inc(v_kept, 1)
                act.wait_ge(q_done, s.n + 1)
                nc.scalar.activation(QT[:, bass.ds(s.n * GW, GW)], bank(2 + s.r), ACT.Identity, bias=BQK[:, 0:1]).then_inc(q_kept, 1)
            steps(act, 0, NG + 1, 2, keep, peel=4, tail=1)

            def softmax(s):
                whole = not isinstance(s.n, int)
                for i in range(4):
                    j = s.batch(M_CEN + i)
                    if j is not None:
                        act.wait_ge(mv2, j + 1)
                        need(act, xt2_done, 4 * j - 3 + i)
                        for t in (2 * i, 2 * i + 1):
                            last = nc.scalar.activation(XC[:, t, :], X[:, bass.ds(j * ST + t, 1), 0:D].rearrange("p a d -> p (a d)"),
                                                        ACT.Identity, bias=MINUS[:, t:t + 1])
                        last.then_inc(xc_done, 1)
                for i in range(4):
                    all_now, alone = s.last_batch(M_TR + 1), s.last_batch(M_TR + 1 + i)
                    j = NS - 1 if all_now else None if alone else s.batch(M_TR + 1 + i)
                    if j is not None:
                        act.wait_ge(xt2_done, 4 * j + i + 1)
                        need(act, lgp_done, 4 * j - 3 + i)
                        nc.scalar.copy(X1T[:, i].rearrange("p t d -> p (t d)"), bank(tr_bank(j, i))[:, 0:2 * P]).then_inc(x1t_ready, 1)
                for t in range(ST):
                    j = s.batch(M_XR + t // 2)
                    if j is not None:
                        turn = 2 * j + t // 4
                        need(act, routed[t % 4], 16 * turn)
                        act.wait_ge(inv_step, INV_STEPS * (j + 1))
                        nc.scalar.copy(XR[:, t % 4, :], X[:, bass.ds(j * ST + t, 1), :].rearrange("p a w -> p (a w)")).then_inc(xr_ready, 1)
                if whole or 1 <= s.n < NT + 1:
                    b = s.back(1)
                    act.wait_ge(pt_done, b.n + 1)
                    need(act, od_done, b.n - 1)
                    nc.scalar.copy(PT[:, b.r % 2].rearrange("p a b -> p (a b)"), bank(4, 2)).then_inc(pt_ready, 1)
                if whole or s.n < NT:
                    act.wait_ge(sub_done, s.n + 1)
                    nc.scalar.activation(SB[:, s.r % 2, :], SB[:, s.r % 2, :], ACT.Exp, scale=SCALE).then_inc(exp_done, 1)
            steps(act, 0, STEPS, ST, softmax, peel=32, tail=STEPS - NT)

            act.wait_ge(we_in, 16)
            act.wait_ge(tab_ready, 1)
            def ffn(s):
                whole = not isinstance(s.n, int)
                if whole or 1 <= s.n < NB + 1:
                    b = s.back(1)
                    act.wait_ge(bx_done, b.n + 1)
                    need(act, h_done, b.n - 1)
                    nc.scalar.copy(XT[:, b.r % 2, :], bank(b.r % 2)[:, 0:P]).then_inc(bxt_ready, 1)
                if whole or s.n < NB:
                    need(act, h_done, s.n - 3)
                    need(act, yx_done, s.n - 3)
                    ex = act.value_load(TABI[0:1, 1, bass.ds(s.n, 1)], min_val=0, max_val=E - 1)
                    nc.scalar.copy(WS[:, s.r % 4, :], WE[:, bass.ds(ex, 1), :].rearrange("p e f -> p (e f)")).then_inc(ws_ready, 1)
                if whole or s.n >= 2:
                    b = s.back(2)
                    act.wait_ge(hb_done, b.n + 1)
                    nc.scalar.activation(HT[:, b.r % 2, :], HT[:, b.r % 2, :], ACT.Relu).then_inc(h_ready, 1)
            steps(act, 0, NB + 2, RR, ffn, peel=RR, tail=2)

        @block.vector
        def _(dve):
            def moments(n, st, ms, mean, minus, var, half, gap, mv, var_read):
                m0, m1, v0, v1 = (st[:, :, k] for k in (1, 4, 2, 5))
                need(dve, mv, n)
                nc.vector.tensor_tensor(ms[:, 0, :], m0, m1, ALU.add)
                nc.vector.tensor_tensor(ms[:, 1, :], v0, v1, ALU.add)
                nc.vector.tensor_tensor(ms[:, 2, :], m0, m1, ALU.subtract).then_inc(half, 1)
                dve.wait_ge(half, n + 1)
                need(dve, *var_read)
                nc.vector.tensor_scalar(mean, ms[:, 0, :], 0.5, None, ALU.mult)
                if minus is not None:
                    nc.vector.tensor_scalar(minus, ms[:, 0, :], -0.5, None, ALU.mult)
                nc.vector.scalar_tensor_tensor(ms[:, 3, :], ms[:, 2, :], 0.25, ms[:, 2, :], ALU.mult, ALU.mult).then_inc(gap, 1)
                dve.wait_ge(gap, n + 1)
                nc.vector.scalar_tensor_tensor(var, ms[:, 1, :], 1.0 / D, ms[:, 3, :], ALU.mult, ALU.add).then_inc(mv, 1)

            def inverse(n, inv, root, sd, rstd, done):
                need(dve, done, n)
                dve.wait_ge(sd, n + 1)
                nc.vector.reciprocal(inv, root).then_inc(rstd, 1)
                dve.wait_ge(rstd, n + 1)

            def normalise(dst, src, mean, inv):
                return nc.vector.tensor_scalar(dst, src, mean, inv, ALU.subtract, ALU.mult)

            def stage1(s):
                whole = not isinstance(s.n, int)
                if whole or s.n < NG:
                    dve.wait_ge(x_in[s.r], 16 * (s.it + 1))
                    xg = X[:, bass.ds(s.n * GT, GT), 0:D]
                    need(dve, half_done, s.n)
                    for t in range(GT):
                        last = nc.vector.bn_stats(STAT[:, t, :], xg[:, t, :])
                    last.then_inc(stat_done, 1)
                    dve.wait_ge(stat_done, s.n + 1)
                    need(dve, xn_done, s.n - 1)
                    moments(s.n, STAT, MS, MV[:, s.r % 2, 0, :], None, MV[:, s.r % 2, 1, :], half_done, gap_done, mv_done, (sd_done, s.n - 1))
                if whole or 1 <= s.n < NG + 1:
                    b = s.back(1)
                    need(dve, xt_done, b.n - 1)
                    xb = X[:, bass.ds(b.n * GT, GT), 0:D]
                    inverse(b.n, RSTD[:], SD[:, b.r % 2, :], sd_done, rstd_done, xn_done)
                    for t in range(GT):
                        last = normalise(XN[:, b.r % 2, t, :], xb[:, t, :], MV[:, b.r % 2, 0, t:t + 1], RSTD[:, t:t + 1])
                    last.then_inc(xn_done, 1)
                if not whole and s.n == 1:
                    dve.wait_ge(w_in, 16)
                    dve.wait_ge(bo_mm, 1)
                    nc.vector.tensor_tensor(BO, bank(7)[:, 0:D], BO, ALU.add).then_inc(bo_ready, 1)
            steps(dve, 0, NG + 1, 4, stage1, peel=4, tail=1)

            nc.vector.memset(HOT[:, ST, :], 0.0).then_inc(zero_row, 1)
            nc.vector.tensor_copy(COUNT[:].rearrange("p a b -> p (a b)"), C[:, C_TRI:C_TRI + 2 * P]).then_inc(zero_row, 1)
            nc.vector.tensor_copy(BASE[:], C[:, C_BASE:C_BASE + E]).then_inc(base_carry, 1)
            def stage3_early(s):
                j = s.batch(M_TOP)
                if j is not None:
                    need(dve, dest_done, j)
                    need(dve, hot_done, j)
                    dve.wait_ge(lgp_done, 4 * j + 4)
                    dve.wait_ge(inv_step, INV_STEPS * (j + 1))
                    nc.vector.tensor_tensor(PREF[:], bank(7)[:, 2 * P:2 * P + ST * E].rearrange("p (t e) -> p t e", e=E),
                                            X[:, bass.ds(j * ST, ST), RS:RS + 1].to_broadcast([P, ST, E]), ALU.mult).then_inc(scaled, 1)
                    dve.wait_ge(scaled, j + 1)
                    nc.vector.tensor_tensor(LG[:], PREF[:], BR.unsqueeze(1).to_broadcast([P, ST, E]), ALU.add).then_inc(lg_ready, 1)
                    dve.wait_ge(lg_ready, j + 1)
                    nc.vector.tensor_reduce(TOP[:], LG[:], axis=AX.X, op=ALU.max).then_inc(top_done, 1)
                    dve.wait_ge(top_done, j + 1)
                    nc.vector.tensor_tensor(PREF[:], LG[:], TOP[:].unsqueeze(2).to_broadcast([P, ST, E]), ALU.is_ge).then_inc(eq_done, 1)
                j = s.batch(M_HOT)
                if j is not None:
                    dve.wait_ge(eq_done, j + 1)
                    nc.vector.tensor_tensor(LG[:], PREF[:], C[:, C_PREF:C_PREF + E].unsqueeze(1).to_broadcast([P, ST, E]), ALU.mult).then_inc(pref_done, 1)
                    dve.wait_ge(pref_done, j + 1)
                    nc.vector.tensor_reduce(TOP[:], LG[:], axis=AX.X, op=ALU.max).then_inc(best_done, 1)
                    dve.wait_ge(best_done, j + 1)
                    need(dve, rank_done, j)
                    need(dve, posm_done, j)
                    nc.vector.tensor_tensor(HOT[:, 0:ST, :], LG[:], TOP[:].unsqueeze(2).to_broadcast([P, ST, E]), ALU.is_ge).then_inc(hot_done, 1)
                j = s.batch(M_POS)
                if j is not None:
                    dve.wait_ge(rank_done, j + 1)
                    dve.wait_ge(base_carry, j + 1)
                    dve.wait_ge(hot_done, j + 1)
                    need(dve, posm_done, j)
                    nc.vector.tensor_tensor(POS[:], bank(7)[:, RK:RK + (ST + 1) * E].rearrange("p (t e) -> p t e", e=E),
                                            BASE[:].unsqueeze(1).to_broadcast([P, ST + 1, E]), ALU.add).then_inc(pos_done, 1)
                    dve.wait_ge(pos_done, j + 1)
                    nc.vector.tensor_copy(BASE[:], POS[:, ST, :]).then_inc(base_carry, 1)
                    nc.vector.tensor_tensor(LG[:], POS[:, 0:ST, :], HOT[:, 0:ST, :], ALU.mult).then_inc(posm_done, 1)
                    dve.wait_ge(posm_done, j + 1)
                    need(dve, desti_done, j)
                    nc.vector.tensor_reduce(DEST[:], LG[:], axis=AX.X, op=ALU.add).then_inc(dest_done, 1)

            def stage2(s):
                whole = not isinstance(s.n, int)
                stage3_early(s)
                if whole or 3 <= s.n < NT + 3:
                    b = s.back(3)
                    dve.wait_ge(wo_done, b.n + 1)
                    xt = X[:, bass.ds(b.n, 1), 0:D].rearrange("p a d -> p (a d)")
                    nc.vector.tensor_tensor(xt, bank(6)[:, 0:128], xt, ALU.add).then_inc(x1_done, 1)
                if whole or s.n < NT:
                    sc = bank(2 * (s.r % 2), 2).rearrange("p (h k) -> p h k", h=H)
                    need(dve, sub_done, s.n - 1)
                    dve.wait_ge(s_done, s.n + 1)
                    nc.vector.tensor_reduce(MX[:, s.r % 2, :], sc, axis=AX.X, op=ALU.max).then_inc(mx_done, 1)
                    dve.wait_ge(mx_done, s.n + 1)
                    need(dve, pt_done, s.n - 1)
                    nc.vector.tensor_tensor(SB[:, s.r % 2].rearrange("p (h k) -> p h k", h=H), sc,
                                            MX[:, s.r % 2, :].unsqueeze(2).to_broadcast([P, H, SEQ]), ALU.subtract).then_inc(sub_done, 1)
                if whole or 2 <= s.n < NT + 2:
                    b = s.back(2)
                    need(dve, ot_ready, b.n)
                    if whole:
                        dve.wait_ge(x1_done, s.n - 3)
                    dve.wait_ge(od_done, b.n + 1)
                    nc.vector.reciprocal(RD[:], bank(6)[:, 128:256]).then_inc(rd_done, 1)
                    dve.wait_ge(rd_done, b.n + 1)
                    need(dve, wo_done, b.n - 1)
                    nc.vector.tensor_tensor(OT[:, b.r % 2, :], bank(6)[:, 0:128], RD[:], ALU.mult).then_inc(ot_ready, 1)
                stage3_late(s)

            def stage3_late(s):
                for t in range(ST):
                    j = s.batch(M_BN + t)
                    if j is not None:
                        if isinstance(s.n, int):
                            dve.wait_ge(x1_done, j * ST + t + 1)
                        x1 = X[:, bass.ds(j * ST + t, 1), 0:D].rearrange("p a d -> p (a d)")
                        nc.vector.bn_stats(STAT2[:, t, :], x1).then_inc(stat2, 1)
                j = s.batch(M_MOM)
                if j is not None:
                    dve.wait_ge(stat2, ST * j + ST)
                    need(dve, xc_done, 4 * j)
                    moments(j, STAT2, MS2, X[:, bass.ds(j * ST, ST), MU], MINUS[:], VAR2[:], half2, gap2, mv2, (inv_step, INV_STEPS * j))
                j = s.batch(M_SEED)
                if j is not None:
                    dve.wait_ge(mv2, j + 1)
                    nc.vector.tensor_scalar(VAR2[:], VAR2[:], EPS, None, ALU.add).then_inc(seed_step, 1)
                    dve.wait_ge(seed_step, 4 * j + 1)
                    nc.vector.tensor_scalar(YY[:].bitcast(i32), VAR2[:].bitcast(i32), 1, None, ALU.logical_shift_right).then_inc(seed_step, 1)
                    dve.wait_ge(seed_step, 4 * j + 2)
                    nc.vector.tensor_scalar(Y[:].bitcast(i32), YY[:].bitcast(i32), -1.0, float(0x5f3759df), ALU.mult, ALU.add).then_inc(seed_step, 1)
                    dve.wait_ge(seed_step, 4 * j + 3)
                    nc.vector.tensor_scalar(HALF[:], VAR2[:], 0.5, None, ALU.mult).then_inc(seed_step, 1)
                    dve.wait_ge(seed_step, 4 * j + 4)

            dve.wait_ge(xb_done, NG)
            steps(dve, 0, STEPS, ST, stage2, peel=32, tail=STEPS - NT)

            for r in range(KR):
                dve.wait_ge(qs_in[r], 16 * (NT // KR))
            dve.wait_ge(vp_done, NT)
            dve.wait_ge(base_carry, NS + 1)
            nc.vector.tensor_copy(CNTI[:], BASE[0:1, :]).then_inc(cnt_ready, 1)
            made = [0]

            def link(ins):
                made[0] += 1
                ins.then_inc(tab_step, 1)
                dve.wait_ge(tab_step, made[0])

            def row(k):
                return TE[0:1, k, :]
            link(nc.vector.tensor_tensor(row(0), BASE[0:1, :], C[0:1, C_BASE:C_BASE + E], ALU.subtract))
            cm = CMP[0:1, 0:E * NT].rearrange("p (e m) -> p e m", e=E)
            link(nc.vector.tensor_tensor(cm, row(0).unsqueeze(2).to_broadcast([1, E, NT]),
                                         C[0:1, C_LIM:C_LIM + NT].unsqueeze(1).to_broadcast([1, E, NT]), ALU.is_gt))
            link(nc.vector.tensor_reduce(row(1), cm, axis=AX.X, op=ALU.add))
            src, dst = 1, 2
            for d in (1, 2, 4):
                link(nc.vector.tensor_copy(TE[0:1, dst, 0:d], TE[0:1, src, 0:d]))
                link(nc.vector.tensor_tensor(TE[0:1, dst, d:E], TE[0:1, src, d:E], TE[0:1, src, 0:E - d], ALU.add))
                src, dst = dst, dst + 1
            past = CMP[0:1, :].rearrange("p (i e) -> p i e", e=E)
            link(nc.vector.tensor_tensor(past, C[0:1, C_BLK:C_BLK + NB].unsqueeze(2).to_broadcast([1, NB, E]),
                                         row(src).unsqueeze(1).to_broadcast([1, NB, E]), ALU.is_ge))
            link(nc.vector.tensor_reduce(TB[0:1, 0, :], past, axis=AX.X, op=ALU.add))
            link(nc.vector.tensor_tensor(past, past, row(1).unsqueeze(1).to_broadcast([1, NB, E]), ALU.mult))
            link(nc.vector.tensor_reduce(TB[0:1, 1, :], past, axis=AX.X, op=ALU.add))
            link(nc.vector.tensor_tensor(TB[0:1, 2, :], C[0:1, C_BLK:C_BLK + NB], TB[0:1, 1, :], ALU.subtract))
            link(nc.vector.tensor_scalar(TB[0:1, 1, :], TB[0:1, 0, :], float(CAP), None, ALU.mult))
            link(nc.vector.scalar_tensor_tensor(TB[0:1, 3, :], TB[0:1, 2, :], float(P), TB[0:1, 1, :], ALU.mult, ALU.add))
            link(nc.vector.tensor_copy(TABI[:, 0, :], TB[0:1, 3, :]))
            link(nc.vector.tensor_scalar(TB[0:1, 2, :], TB[0:1, 0, :], float(E - 1), None, ALU.min))
            nc.vector.tensor_copy(TABI[:, 1, :], TB[0:1, 2, :]).then_inc(tab_ready, 1)

            def ffn(s):
                whole = not isinstance(s.n, int)
                if whole or s.n < NB:
                    need(dve, bx_done, s.n - 3)
                    dve.wait_ge(rt_in[s.r], 16 * (s.it + 1))
                    nc.vector.tensor_scalar(RN[:, s.r % 4, :], RT[:, s.r, 0:D], RT[:, s.r, MU:MU + 1], RT[:, s.r, RS:RS + 1],
                                            ALU.subtract, ALU.mult).then_inc(rn_done, 1)
                if whole or 2 <= s.n < NB + 2:
                    b = s.back(2)
                    dve.wait_ge(h_done, b.n + 1)
                    need(dve, y_done, b.n - 1)
                    nc.vector.tensor_tensor(HT[:, b.r % 2, :].rearrange("p (c t) -> p c t", c=FC),
                                            bank(2 + b.r % 2).rearrange("p (c t) -> p c t", c=FC),
                                            WS[:, b.r % 4, F:F + FC].unsqueeze(2).to_broadcast([P, FC, P]),
                                            ALU.add).then_inc(hb_done, 1)
                if whole or s.n >= 3:
                    b = s.back(3)
                    need(dve, y_out[b.r], 16 * b.it)
                    dve.wait_ge(y_done, b.n + 1)
                    nc.vector.tensor_tensor(YO[:, b.r, :], bank(4 + b.r % 2)[:, 0:D],
                                            WS[:, b.r % 4, F + FC:WEW], ALU.add).then_inc(yx_done, 1)
                    dve.wait_ge(yx_done, b.n + 1)
                    nc.vector.tensor_tensor(YO[:, b.r, :], YO[:, b.r, :], RT[:, b.r, 0:D], ALU.add).then_inc(yo_ready, 1)
            steps(dve, 0, NB + 3, RR, ffn, peel=RR, tail=3)

        @block.tensor
        def _(pe):
            pe.wait_ge(con_in, 16)
            pe.wait_ge(w_in, 16)
            nc.tensor.matmul(bank(7)[:, 0:D], BV, WO, start=True, stop=True).then_inc(bo_mm, 1)

            def stage1(s):
                pe.wait_ge(ct_in[s.r], 16 * (s.it + 1))
                need(pe, k_kept, s.n - 1)
                nc.tensor.matmul(bank(4 + s.r % 2), WK, CT[:, s.r, :], start=True, stop=True).then_inc(k_done, 1)
                pe.wait_ge(xn_done, s.n + 1)
                need(pe, xnt_ready, s.n - 1)
                for t in range(GT):
                    last = nc.tensor.transpose(bank(s.r % 2)[:, t * P:(t + 1) * P], XN[:, s.r % 2, t, :], ident)
                last.then_inc(xt_done, 1)
                need(pe, v_kept, s.n - 1)
                if isinstance(s.n, int) and s.n == 1:
                    pe.wait_ge(bo_ready, 1)
                for b in range(2 * GT):
                    for r in range(2):
                        h = slice(SEQ * r, SEQ * r + SEQ)
                        last = nc.tensor.matmul(bank(6 + s.r % 2)[h, b * SEQ:(b + 1) * SEQ], CT[:, s.r, b * SEQ:(b + 1) * SEQ],
                                                WV[:, h], start=True, stop=True)
                last.then_inc(v_done, 1)
                pe.wait_ge(xnt_ready, s.n + 1)
                need(pe, q_kept, s.n - 1)
                nc.tensor.matmul(bank(2 + s.r % 2), WQ, XNT[:, s.r % 2, :], start=True, stop=True).then_inc(q_done, 1)
            steps(pe, 0, NG, 4, stage1, peel=4)

            pe.wait_ge(q_kept, NG)
            pe.wait_ge(v_kept, NG)
            ob = C[:, C_OB:C_OB + 64].rearrange("p (s m) -> p s m", s=2)

            def feature_major(j, i):
                pe.wait_ge(xc_done, 4 * j + i + 1)
                for t in range(2):
                    last = nc.tensor.transpose(bank(tr_bank(j, i))[:, t * P:(t + 1) * P], XC[:, 2 * i + t, :], ident)
                last.then_inc(xt2_done, 1)

            def project(b):
                pe.wait_ge(ot_ready, b.n + 1)
                nc.tensor.matmul(bank(6)[:, 0:128], OT[:, b.r % 2, :], WO, start=True, stop=True).then_inc(wo_done, 1)

            def stage2(s):
                whole = not isinstance(s.n, int)
                if whole or s.n < NT:
                    pe.wait_ge(qs_in[s.r % KR], 16 * s.turn(KR))
                    pe.wait_ge(km_in[s.r % KR], 64 * s.turn(KR))
                    need(pe, sub_done, s.n - 1)
                    for half in range(2):
                        for b in range(2):
                            if half and b and (whole or s.n >= 3):
                                project(s.back(3))
                            q = QS[:, s.r % KR, SEQ * b:SEQ * b + SEQ]
                            k = KM[:, s.r % KR, b, 8 * half:8 * half + 8, :]
                            last = nc.tensor.matmul(bank(2 * (s.r % 2) + half)[SEQ * b:SEQ * b + SEQ, :], q, k, start=True, stop=True)
                    last.then_inc(s_done, 1)
                elif s.n < NT + 3:
                    project(s.back(3))
                if whole or 1 <= s.n < NT + 1:
                    b1 = s.back(1)
                    pe.wait_ge(exp_done, b1.n + 1)
                    need(pe, pt_ready, b1.n)
                    for hp in range(HP):
                        last = nc.tensor.transpose(bank(4, 2)[:, hp * P:(hp + 1) * P], SB[:, b1.r % 2, hp * P:(hp + 1) * P], ident)
                    last.then_inc(pt_done, 1)
                if whole or 2 <= s.n < NT + 2:
                    b2 = s.back(2)
                    pe.wait_ge(pt_ready, b2.n + 1)
                    pe.wait_ge(vp_done, b2.n + 1)
                    need(pe, x1_done, b2.n)
                    for b in range(2):
                        for z in range(2):
                            for c in range(4):
                                nc.tensor.matmul(bank(6)[32 * c:32 * c + 32, SEQ * b:SEQ * b + SEQ],
                                                 VP[:, b2.r % 2, b, 2 * c + z, :], PT[:, b2.r % 2, 2 * c + z, SEQ * b:SEQ * b + SEQ],
                                                 start=z == 0, stop=z == 1)
                    for z in range(2):
                        for c in range(4):
                            last = nc.tensor.matmul(bank(6)[32 * c:32 * c + 32, P:2 * P], ob[:, z, :],
                                                    PT[:, b2.r % 2, 2 * c + z, :], start=z == 0, stop=z == 1)
                    last.then_inc(od_done, 1)

                for i in range(4):
                    j = s.batch(M_LG + i)
                    if j is not None:
                        pe.wait_ge(x1t_ready, 4 * j + i + 1)
                        if i == 0:
                            need(pe, pos_done, j)
                        for t in range(2):
                            at = 2 * P + (2 * i + t) * E
                            last = nc.tensor.matmul(bank(7)[:, at:at + E], X1T[:, i, t, :], WR, start=True, stop=True)
                        last.then_inc(lgp_done, 1)
                for i in range(4):
                    j = s.batch(M_TR + i)
                    if j is None or s.last_batch(M_TR + i):
                        continue
                    need(pe, x1t_ready, 4 * j + i)
                    if i == 0:
                        need(pe, pos_done, j)
                    feature_major(j, i)
                if s.last_batch(M_TR):
                    pe.wait_ge(sub_done, NT)
                    for i in range(4):
                        feature_major(NS - 1, i)
                j = s.batch(M_RANK)
                if j is not None:
                    pe.wait_ge(hot_done, j + 1)
                    sums = bank(7)[:, RK:RK + (ST + 1) * E]
                    nc.tensor.matmul(sums, COUNT[:, 0, :], HOT[:].rearrange("p t e -> p (t e)"), start=True, stop=False)
                    for t in range(ST):
                        last = nc.tensor.matmul(sums[:, (t + 1) * E:].rearrange("p (t e) -> p t e", e=E), COUNT[:, 1, :],
                                                HOT[:, t:t + 1, :].to_broadcast([P, ST - t, E]), start=False, stop=t == ST - 1)
                    last.then_inc(rank_done, 1)
            pe.wait_ge(zero_row, 2)
            steps(pe, 0, STEPS, ST, stage2, peel=24, tail=STEPS - NT)
            pe.wait_ge(sub_done, NT)
            pe.wait_ge(pt_ready, NT)

            pe.wait_ge(w2_in, 16)
            pe.wait_ge(tab_ready, 1)

            def transpose_rows(s):
                pe.wait_ge(rn_done, s.n + 1)
                need(pe, bxt_ready, s.n - 1)
                nc.tensor.transpose(bank(s.r % 2)[:, 0:P], RN[:, s.r % 4, :], ident).then_inc(bx_done, 1)

            def ffn(s):
                whole = not isinstance(s.n, int)
                def expert():
                    return pe.value_load(TABI[0:1, 1, bass.ds(s.back(2).n, 1)], min_val=0, max_val=E - 1)
                if whole or s.n < NB:
                    transpose_rows(s)
                if whole or 1 <= s.n < NB + 1:
                    b = s.back(1)
                    pe.wait_ge(bxt_ready, b.n + 1)
                    pe.wait_ge(ws_ready, b.n + 1)
                    need(pe, hb_done, b.n - 1)
                    for c in range(FC):
                        last = nc.tensor.matmul(bank(2 + b.r % 2)[:, c * P:(c + 1) * P], WS[:, b.r % 4, c * P:(c + 1) * P],
                                                XT[:, b.r % 2, :], start=True, stop=True)
                        if c == 1 and (whole or s.n >= 2):
                            ex = expert()
                    last.then_inc(h_done, 1)
                elif s.n >= 2:
                    ex = expert()
                if whole or s.n >= 2:
                    b = s.back(2)
                    pe.wait_ge(h_ready, b.n + 1)
                    need(pe, yx_done, b.n - 1)
                    for c in range(FC):
                        w = W2[:, bass.ds(ex, 1), c, :].rearrange("p a d -> p (a d)")
                        last = nc.tensor.matmul(bank(4 + b.r % 2)[:, 0:D], HT[:, b.r % 2, c * P:(c + 1) * P], w,
                                                start=c == 0, stop=c == FC - 1)
                    last.then_inc(y_done, 1)
            steps(pe, 0, NB + 2, RR, ffn, peel=RR, tail=2)


def kernel(x, ctx_1024, L0_xattn_Wq, L0_xattn_bq, L0_xattn_Wk, L0_xattn_bk, L0_xattn_Wv, L0_xattn_bv,
           L0_xattn_Wo, L0_xattn_bo, L0_ffn_Wr, L0_ffn_br, L0_ffn_W1, L0_ffn_b1, L0_ffn_W2, L0_ffn_b2):
    import concourse.bacc as bacc
    from concourse.bass_utils import run_bass_kernel_spmd

    def lay(a):
        return np.ascontiguousarray(a)

    con, pad, ids = constants()
    n = np.asarray
    arrays = {
        "x": lay(n(x).reshape(TOK, D)),
        "ctxT": lay(n(ctx_1024).reshape(TOK, D).T),
        "wts": lay(np.concatenate([
            n(L0_xattn_Wq).T, n(L0_xattn_Wk).T,
            n(L0_xattn_Wv).reshape(HP, 2, DK, D).transpose(3, 1, 0, 2).reshape(D, D),
            n(L0_xattn_bq)[:, None], n(L0_xattn_bk)[:, None], n(L0_xattn_Wo).T,
            np.broadcast_to(n(L0_xattn_bv)[:, None], (D, P)), np.broadcast_to(n(L0_xattn_bo)[None], (P, D)),
            n(L0_ffn_Wr).T, np.broadcast_to(n(L0_ffn_br)[None], (P, E))], axis=1)),
        "we": lay(np.concatenate([n(L0_ffn_W1).transpose(2, 0, 1), n(L0_ffn_b1).reshape(E, FC, P).transpose(2, 0, 1),
                                  np.broadcast_to(n(L0_ffn_b2)[None], (P, E, D))], axis=2)),
        "w2": lay(n(L0_ffn_W2).reshape(E, D, FC, P).transpose(3, 0, 2, 1)),
        "con": con, "pad": pad, "ids": ids,
    }
    nc = bacc.Bacc("TRN2", target_bir_lowering=False, num_devices=1)
    args = [nc.dram_tensor("in_" + k, a.shape, mybir.dt.from_np(a.dtype), kind="ExternalInput").ap()
            for k, a in arrays.items()]
    out = nc.dram_tensor("out", (TOK, D), mybir.dt.float32, kind="ExternalOutput").ap()
    build(nc, *args, out)
    r = run_bass_kernel_spmd(nc, [{"in_" + k: a for k, a in arrays.items()}], core_ids=[0])
    return r.results[0]["out"].reshape(BATCH, SEQ, D)
```
